# Optimizing a Trainium2 kernel written in Bass

```python
import numpy as np
import jax
import jax.numpy as jnp

def _softmax(x, axis=-1):
    return jax.nn.softmax(x, axis=axis)

def _gelu(x):
    return jax.nn.gelu(x, approximate=True)

def _silu(x):
    return jax.nn.silu(x)

def _sigmoid(x):
    return jax.nn.sigmoid(x)

def _layernorm(x, axis=-1, eps=1e-05):
    m = jnp.mean(x, axis=axis, keepdims=True)
    v = jnp.var(x, axis=axis, keepdims=True)
    return (x - m) / jnp.sqrt(v + eps)

def _scatter_add(tgt, idx, src, axis=0):
    return tgt.at[idx].add(src)

def _segment_sum(src, seg, n):
    return jax.ops.segment_sum(src, seg, n)
kernel_name = 'mk_seq_postln_d1_jaxref_r8_976042'

def setup_inputs(seed: int=0):
    np.random.seed(seed)
    _w = jnp.asarray

    def _L0_attn_setup():
        import jax, jax.numpy as jnp
        import numpy as np
        import math
        EMBED_DIM = 128
        NUM_HEADS = 16
        HEAD_DIM = EMBED_DIM // NUM_HEADS // 2
        DEPTH = 12
        LAMBDA_INIT = 0.8 - 0.6 * math.exp(-0.3 * DEPTH)
        RMS_EPS = 1e-05
        key = jax.random.key(seed)
        ks = jax.random.split(key, 10)
        B, S, E = (2, 128, EMBED_DIM)
        w_std = 0.02
        x = jax.random.normal(ks[0], (B, S, E), dtype=jnp.float32)
        Wq = jax.random.normal(ks[1], (E, E), dtype=jnp.float32) * w_std
        Wk = jax.random.normal(ks[2], (E, E), dtype=jnp.float32) * w_std
        Wv = jax.random.normal(ks[3], (E, E), dtype=jnp.float32) * w_std
        Wo = jax.random.normal(ks[4], (E, E), dtype=jnp.float32) * w_std
        lq1 = jax.random.normal(ks[5], (HEAD_DIM,), dtype=jnp.float32) * 0.1
        lk1 = jax.random.normal(ks[6], (HEAD_DIM,), dtype=jnp.float32) * 0.1
        lq2 = jax.random.normal(ks[7], (HEAD_DIM,), dtype=jnp.float32) * 0.1
        lk2 = jax.random.normal(ks[8], (HEAD_DIM,), dtype=jnp.float32) * 0.1
        rms_w = jnp.ones((2 * HEAD_DIM,), dtype=jnp.float32)
        return {'x': x, 'Wq': Wq, 'Wk': Wk, 'Wv': Wv, 'Wo': Wo, 'lq1': lq1, 'lk1': lk1, 'lq2': lq2, 'lk2': lk2, 'rms_w': rms_w}
    _L0_attn_in = _L0_attn_setup()

    def _L0_ffn_setup():
        import jax, jax.numpy as jnp
        import numpy as np
        DIM = 128

        def _reference_tuple_inner(x, W_r, W_k, W_v, mu_r, mu_k):
            B, T, C = x.shape
            x_prev = jnp.concatenate([jnp.zeros((B, 1, C), x.dtype), x[:, :-1, :]], axis=1)
            xr = mu_r * x + (1.0 - mu_r) * x_prev
            xk = mu_k * x + (1.0 - mu_k) * x_prev
            r = jax.nn.sigmoid(jnp.einsum('btc,dc->btd', xr, W_r))
            k = jnp.einsum('btc,dc->btd', xk, W_k)
            k_act = jnp.square(jax.nn.relu(k))
            out = r * jnp.einsum('btc,dc->btd', k_act, W_v)
            new_state = x[:, -1, :]
            return (out, new_state)
        key = jax.random.key(seed)
        ks = jax.random.split(key, 6)
        B, T, C = (8, 256, DIM)
        x = jax.random.normal(ks[0], (B, T, C), dtype=jnp.float32)
        s = 1.0 / np.sqrt(C)
        W_r = jax.random.uniform(ks[1], (C, C), jnp.float32, -s, s)
        W_k = jax.random.uniform(ks[2], (C, C), jnp.float32, -s, s)
        W_v = jax.random.uniform(ks[3], (C, C), jnp.float32, -s, s)
        mu_r = jax.random.uniform(ks[4], (C,), jnp.float32)
        mu_k = jax.random.uniform(ks[5], (C,), jnp.float32)
        return {'x': x, 'W_r': W_r, 'W_k': W_k, 'W_v': W_v, 'mu_r': mu_r, 'mu_k': mu_k}
    _L0_ffn_in = _L0_ffn_setup()
    _d = {'L0_attn_x': _L0_attn_in['x'], 'L0_attn_Wq': _L0_attn_in['Wq'], 'L0_attn_Wk': _L0_attn_in['Wk'], 'L0_attn_Wv': _L0_attn_in['Wv'], 'L0_attn_Wo': _L0_attn_in['Wo'], 'L0_attn_lq1': _L0_attn_in['lq1'], 'L0_attn_lk1': _L0_attn_in['lk1'], 'L0_attn_lq2': _L0_attn_in['lq2'], 'L0_attn_lk2': _L0_attn_in['lk2'], 'L0_attn_rms_w': _L0_attn_in['rms_w'], 'L0_ffn_W_r': _L0_ffn_in['W_r'], 'L0_ffn_W_k': _L0_ffn_in['W_k'], 'L0_ffn_W_v': _L0_ffn_in['W_v'], 'L0_ffn_mu_r': _L0_ffn_in['mu_r'], 'L0_ffn_mu_k': _L0_ffn_in['mu_k']}
    _x0 = _d['L0_attn_x']
    _d['L0_attn_x'] = jax.random.normal(jax.random.fold_in(jax.random.key(seed), 1), (2, 1024, 128), dtype=_x0.dtype)
    del _x0
    return _d

def reference(L0_attn_x, L0_attn_Wq, L0_attn_Wk, L0_attn_Wv, L0_attn_Wo, L0_attn_lq1, L0_attn_lk1, L0_attn_lq2, L0_attn_lk2, L0_attn_rms_w, L0_ffn_W_r, L0_ffn_W_k, L0_ffn_W_v, L0_ffn_mu_r, L0_ffn_mu_k):

    def _L0_attn_ref(x, Wq, Wk, Wv, Wo, lq1, lk1, lq2, lk2, rms_w):
        import jax, jax.numpy as jnp
        import numpy as np
        import math
        EMBED_DIM = 128
        NUM_HEADS = 16
        HEAD_DIM = EMBED_DIM // NUM_HEADS // 2
        DEPTH = 12
        LAMBDA_INIT = 0.8 - 0.6 * math.exp(-0.3 * DEPTH)
        RMS_EPS = 1e-05
        B, S, E = x.shape
        H, d = (NUM_HEADS, HEAD_DIM)
        scaling = d ** (-0.5)
        q = (x @ Wq).reshape(B, S, 2 * H, d).transpose(0, 2, 1, 3) * scaling
        k = (x @ Wk).reshape(B, S, 2 * H, d).transpose(0, 2, 1, 3)
        v = (x @ Wv).reshape(B, S, H, 2 * d).transpose(0, 2, 1, 3)
        scores = jnp.einsum('bhqd,bhkd->bhqk', q, k)
        causal_mask = jnp.triu(jnp.ones((S, S), dtype=bool), 1)
        scores = jnp.where(causal_mask, -jnp.inf, scores)
        probs = jax.nn.softmax(scores, axis=-1)
        lam = jnp.exp(jnp.sum(lq1 * lk1)) - jnp.exp(jnp.sum(lq2 * lk2)) + LAMBDA_INIT
        probs = probs.reshape(B, H, 2, S, S)
        attn_weights = probs[:, :, 0] - lam * probs[:, :, 1]
        attn = jnp.einsum('bhqk,bhkd->bhqd', attn_weights, v)
        attn = attn * jax.lax.rsqrt(jnp.mean(attn * attn, axis=-1, keepdims=True) + RMS_EPS) * rms_w
        attn = attn * (1.0 - LAMBDA_INIT)
        out = attn.transpose(0, 2, 1, 3).reshape(B, S, H * 2 * d) @ Wo
        return out

    def _L0_ffn_ref(x, W_r, W_k, W_v, mu_r, mu_k):
        import jax, jax.numpy as jnp
        import numpy as np
        DIM = 128

        def _reference_tuple_inner(x, W_r, W_k, W_v, mu_r, mu_k):
            B, T, C = x.shape
            x_prev = jnp.concatenate([jnp.zeros((B, 1, C), x.dtype), x[:, :-1, :]], axis=1)
            xr = mu_r * x + (1.0 - mu_r) * x_prev
            xk = mu_k * x + (1.0 - mu_k) * x_prev
            r = jax.nn.sigmoid(jnp.einsum('btc,dc->btd', xr, W_r))
            k = jnp.einsum('btc,dc->btd', xk, W_k)
            k_act = jnp.square(jax.nn.relu(k))
            out = r * jnp.einsum('btc,dc->btd', k_act, W_v)
            new_state = x[:, -1, :]
            return (out, new_state)
        return _reference_tuple_inner(x, W_r, W_k, W_v, mu_r, mu_k)[0]
    x = L0_attn_x
    x = _layernorm(x + _L0_attn_ref(x, L0_attn_Wq, L0_attn_Wk, L0_attn_Wv, L0_attn_Wo, L0_attn_lq1, L0_attn_lk1, L0_attn_lq2, L0_attn_lk2, L0_attn_rms_w), axis=-1)
    x = _layernorm(x + _L0_ffn_ref(x, L0_ffn_W_r, L0_ffn_W_k, L0_ffn_W_v, L0_ffn_mu_r, L0_ffn_mu_k), axis=-1)
    return x

_drawn_inputs = setup_inputs


def setup_inputs(seed=0):
    import zlib

    import numpy as np

    out = dict(_drawn_inputs(seed))
    spreads = {'L0_attn_rms_w': (1.0, 0.6)}
    factors = {'L0_attn_Wq': 3.614,
     'L0_attn_Wk': 3.427,
     'L0_attn_lq1': 8.0,
     'L0_attn_lk1': 8.0,
     'L0_attn_lq2': 8.0,
     'L0_attn_lk2': 8.0,
     'L0_ffn_W_r': 3.161,
     'L0_ffn_mu_r': 6.234}
    for name, (base, spread) in spreads.items():
        noise = np.random.default_rng([zlib.crc32(name.encode()), seed]).standard_normal(out[name].shape)
        drawn = base * np.exp(spread * noise) if base else spread * noise
        out[name] = jnp.asarray(drawn.astype(out[name].dtype))
    for name, factor in factors.items():
        out[name] = (out[name] * factor).astype(out[name].dtype)
    return out
```

```python
import math
from contextlib import ExitStack

import concourse.bass as bass
from concourse import mybir

F32 = mybir.dt.float32
BF16 = mybir.dt.bfloat16
ALU = mybir.AluOpType
ACT = mybir.ActivationFunctionType
AX = mybir.AxisListType

P = 128
BANK = 512
HEADS = 16
D = P // HEADS // 2
VW = 2 * D
SUBS = 4
STRIP = 32
LAMBDA_INIT = 0.8 - 0.6 * math.exp(-0.3 * 12)
RMS_EPS = 1e-5
LN_EPS = 1e-5
NEG = -1e30

TERMS = [(0, 0), (0, 1), (1, 0), (1, 1), (0, 2), (2, 0)]
KROWS = len(TERMS) * D
XROWS = KROWS + 2

MAX_UNITS = [
    ([(0, 0, 0, 1), (128, 2, 0, 3)], [0, 384]),
    ([(0, 4, 4, 1), (128, 6, 4, 3)], [0, 384]),
    ([(0, 3, 0, 4)], [384]),
    ([(0, 7, 4, 4)], [384]),
    ([(0, 4, 0, 4)], []),
    ([(0, 5, 0, 4)], []),
    ([(0, 6, 0, 4)], []),
    ([(0, 7, 0, 4)], []),
    ([(0, 1, 0, 2), (256, 5, 4, 2)], [128, 384]),
]
NU = len(MAX_UNITS) * SUBS
RING = NU + 1

QUADS = [
    (0, [(0, 0, 512)]),
    (0, [(1, 0, 384), (3, 384, 128)]),
    (0, [(2, 0, 256)]),
    (1, [(0, 0, 512)]),
    (1, [(1, 0, 512)]),
    (1, [(2, 0, 512)]),
    (1, [(3, 0, 512)]),
    (1, [(4, 0, 512)]),
    (1, [(5, 0, 384), (7, 384, 128)]),
    (1, [(6, 0, 256)]),
]
NQ = len(QUADS)
ESLOTS = 5
DIAG = [[col for kb, col, w in parts if kb // 4 == c] for c, parts in QUADS]
NSEL = sum(map(len, DIAG))
SEL_BY = [sum(map(len, DIAG[: k + 1])) for k in range(NQ)]

EARLY = 11
TQUAD = 7
UNITS_AT = [4, 4, 3, 4, 3, 4, 3, 4, 4, 3]
assert sum(UNITS_AT[:TQUAD]) == NU - EARLY and sum(UNITS_AT[TQUAD:]) == EARLY


def wait(eng, sem, value):
    if isinstance(value, int) and value <= 0:
        return
    eng.wait_ge(sem, value)


def build(nc, x, Wq, Wk, Wv, Wo, lq1, lk1, lq2, lk2, rms_w, W_r, W_k, W_v, mu_r, mu_k, out):
    B, S, _ = x.shape
    NB = S // P
    NT = B * NB
    NCH = NT * P // BANK
    GPB = 2 * HEADS // SUBS
    NG = B * GPB
    NSUB = NG * SUBS
    SCALE = D ** -0.5

    q_rows = nc.dram_tensor("q_rows", (NSUB, STRIP, S), BF16, kind="Internal").ap()
    k_rows = nc.dram_tensor("k_rows", (NSUB, STRIP, S), BF16, kind="Internal").ap()
    w_bounce = nc.dram_tensor("w_bounce", (HEADS, VW), F32, kind="Internal").ap()
    q_group = q_rows.rearrange("(n j) r t -> n (j r) t", j=SUBS)
    k_group = k_rows.rearrange("(n j) r t -> n (j r) t", j=SUBS)
    x_tiles = x.rearrange("b (n p) c -> p (b n) c", p=P)
    out_tiles = out.rearrange("b (n p) c -> p (b n) c", p=P)

    with ExitStack() as ctx:
        def sb(name, shape, dt=F32):
            return ctx.enter_context(nc.sbuf_tensor(name, shape, dt))

        def sem(name):
            return ctx.enter_context(nc.semaphore(name))

        x_tok = sb("x_tok", [P, NT, P])
        xT = sb("xT", [P, NT * P])
        wq_sb, wk_sb, wv_sb, wo_sb = (sb(n, [P, P]) for n in ("wq_sb", "wk_sb", "wv_sb", "wo_sb"))
        wf_sb = sb("wf_sb", [P, 3, P])
        wo_scaled = sb("wo_scaled", [P, P])
        w_cur = sb("w_cur", [P, 2, P])
        w_prev = sb("w_prev", [P, 2, P])
        wvT = sb("wvT", [P, P])
        mu = sb("mu", [P, 2])
        mu1 = sb("mu1", [P, 2])
        rms_col = sb("rms_col", [P, 1])
        rms_scaled = sb("rms_scaled", [P, 1])
        lam_in = sb("lam_in", [P, 4, D])
        lam_prod = sb("lam_prod", [P, 2, D])
        lam_sum = sb("lam_sum", [P, 2])
        lam_exp = sb("lam_exp", [P, 2])
        lam_neg = sb("lam_neg", [P, 1])
        identf = sb("identf", [P, P])
        identb = sb("identb", [P, P], BF16)
        ones_rows = sb("ones_rows", [P, S], BF16)
        mask_zero = sb("mask_zero", [P, 2, P], BF16)
        mask = sb("mask", [P, 2, P], BF16)
        parts = [[sb(f"part_{w}{a}", [P, B, S], BF16) for a in range(3)] for w in "qk"]
        rest = sb("rest", [P, 4, BANK])
        v_all = sb("v_all", [P, NG * NB * 2 * VW])
        v_grp = [sb(f"v_grp{i}", [P, NB, 2, STRIP]) for i in range(2)]
        qm = [sb(f"qm{i}", [P, S], BF16) for i in range(2)]
        km = [sb(f"km{i}", [P, S], BF16) for i in range(2)]
        qe = [sb(f"qe{i}", [P, S], BF16) for i in range(2)]
        ke = [sb(f"ke{i}", [P, S], BF16) for i in range(2)]
        part_max = sb("part_max", [P, SUBS, len(MAX_UNITS), 4])
        far_max = sb("far_max", [P, SUBS, 4])
        row_max = sb("row_max", [P, SUBS, NB])
        neg_max = sb("neg_max", [P, 2, SUBS, NB], BF16)
        max_rows = sb("max_rows", [2 * SUBS, S], BF16)
        e_buf = sb("e_buf", [P, ESLOTS, SUBS, BANK])
        o_rows = [sb(f"o_rows{c}", [P, BANK]) for c in range(2)]
        o_tok = sb("o_tok", [P, NG * NB * SUBS * (VW + 1)])

        ex = [ctx.enter_context(nc.psum_tensor(f"ex{i}", [P, 2, BANK], F32)) for i in range(2)]
        acc = [ctx.enter_context(nc.psum_tensor(f"acc{i}", [P, BANK], F32)) for i in range(2)]
        mx = [ctx.enter_context(nc.psum_tensor(f"mx{i}", [P, BANK], F32)) for i in range(2)]
        wide = [ex[0][:, 0, :], ex[0][:, 1, :], ex[1][:, 0, :], ex[1][:, 1, :]]
        narrow = [acc[0][:], acc[1][:], mx[0][:], mx[1][:]]

        names = """x_in wqk_in wv_in w_in small_in bounce_in
                   ident ones_set mask_set vpad_set xcol_set
                   xt_done xt_copied_a xt_copied_d proj_done hi_done rest_done mid_done lo_done
                   v_done v_copied wt_done wvt_copied wt_scaled lam_dots lam_exped lam_done rms_done
                   rows_b0 rows_b1 qkm_in0 qkm_in1 qke_in0 qke_in1 max_rows_in v_grp_set
                   max_scored maxed combined negmax_done negmax_turned negmax_copied
                   scored exped masked summed acc_copied acc_turned o_stored
                   normed_d attn_ready a_turned a_copied a_projected y_added stats1 x1_ready
                   x1_turned x1_copied k_scored r_scored k_relued r_exped k_squared o_scored z_steps z_ready
                   stats2 rms_rooted rooted1 rooted2 half_set quad_seen out_ready out_stored tail_d""".split()
        s = {n: sem(n) for n in names}
        s_qkm = [s["qkm_in0"], s["qkm_in1"]]
        s_qke = [s["qke_in0"], s["qke_in1"]]

        flat = e_buf[:].rearrange("p s j t -> p (s j t)")

        def reuse(lo, n, pattern, **sizes):
            return flat[:, lo:lo + n].rearrange(pattern, **sizes)

        NM = NG * NB
        o_scaled = reuse(0, NM * SUBS * VW, "p (m j w) -> p m j w", j=SUBS, w=VW)
        attn = reuse(4096, NM * 2 * VW, "p (m h w) -> p m h w", h=2, w=VW)
        attn_sq = reuse(6144, NM * 2 * VW, "p (m h w) -> p m h w", h=2, w=VW)
        attn_n = reuse(8192, NM * 2 * VW, "p (b q g h w) -> p b g q h w", b=B, q=NB, g=GPB, h=2)
        z0 = reuse(0, NT * P, "p (c t) -> p c t", c=NCH)
        z = reuse(2048, NT * P, "p (t c) -> p t c", t=NT)
        res = reuse(4096, NT * P, "p (t c) -> p t c", t=NT)
        r_one = reuse(6144, NT * P, "p (c t) -> p c t", c=NCH)
        y = xT[:].rearrange("p (t c) -> p t c", t=NT)
        r_den = sb("r_den", [P, NM, SUBS])
        ssum = sb("ssum", [P, NM * 2])
        rstd = sb("rstd", [P, NM * 2])
        attnT = sb("attnT", [P, NCH, BANK])
        st1 = sb("st1", [P, NT, 6])
        mv1 = sb("mv1", [P, NT, 2])
        ve1 = sb("ve1", [P, NT])
        rs1 = sb("rs1", [P, NT])
        x1 = sb("x1", [P, NT, P])
        x1T = sb("x1T", [P, B, 1 + S])
        k_relu = sb("k_relu", [P, NCH, BANK])
        k_act = sb("k_act", [P, NCH, BANK])
        r_exp = v_all[:].rearrange("p (c t) -> p c t", c=NCH)
        r_sig = attnT
        st2 = sb("st2", [P, NT, 6])
        mv2 = sb("mv2", [P, NT, 2])
        ve2 = sb("ve2", [P, NT])
        rs2 = sb("rs2", [P, NT])
        minus_half = sb("minus_half", [P, NM * 2])

        block = ctx.enter_context(nc.Block())

        def load_max_rows(sp, n, par):
            wait(sp, s["max_scored"], NU * (n - 1))
            sp.dma_start(qm[par][:], q_group[n]).then_inc(s_qkm[par], 16)
            sp.dma_start(km[par][:], k_group[n]).then_inc(s_qkm[par], 16)

        def load_exp_rows(sp, n, par):
            wait(sp, s["scored"], 2 * NQ * (n - 1))
            sp.dma_start(qe[par][:], q_group[n]).then_inc(s_qke[par], 16)
            sp.dma_start(ke[par][:], k_group[n]).then_inc(s_qke[par], 16)

        def place_maxima(sp, n, par, visit):
            wait(sp, s_qke[par], 32 * (visit + 1))
            wait(sp, s["negmax_copied"], n + 1)
            for e in range(2):
                sp.dma_start(qe[par][KROWS + e:P:STRIP, :], max_rows[SUBS * e:SUBS * (e + 1), :])\
                    .then_inc(s["max_rows_in"], 16)

        @block.sync
        def _(sp):
            sp.dma_start(x_tok[:], x_tiles).then_inc(s["x_in"], 16)
            sp.dma_start(wq_sb[:], Wq).then_inc(s["wqk_in"], 16)
            sp.dma_start(wk_sb[:], Wk).then_inc(s["wqk_in"], 16)
            sp.dma_start(wv_sb[:], Wv).then_inc(s["wv_in"], 16)
            sp.wait_ge(s["ones_set"], 1)
            for b, done in enumerate((s["rows_b0"], s["rows_b1"])):
                subs = slice(b * NSUB // B, (b + 1) * NSUB // B)
                for rows in (q_rows, k_rows):
                    for h in range(2):
                        lo = subs.start + h * P // 8
                        sp.dma_start(rows[lo:lo + P // 8, KROWS:STRIP, :], ones_rows[:]).then_inc(done, 16)
                for part, need in ((0, "hi_done"), (1, "mid_done"), (2, "lo_done")):
                    sp.wait_ge(s[need], 4 * (b + 1))
                    for w, rows in enumerate((q_rows, k_rows)):
                        for t, term in enumerate(TERMS):
                            if term[w] == part:
                                sp.dma_start(rows[subs, D * t:D * (t + 1), :], parts[w][part][:, b, :])\
                                    .then_inc(done, 16)
                if b == 0:
                    sp.wait_ge(done, 16 * (4 + 2 * len(TERMS)))
                    load_max_rows(sp, 0, 0)
                    load_max_rows(sp, 1, 1)
                    load_exp_rows(sp, 0, 0)
            place_maxima(sp, 0, 0, 0)

            def group(n, par, visit):
                if not isinstance(n, int) or n + 2 < NG:
                    load_max_rows(sp, n + 2, par)
                if not isinstance(n, int) or n + 1 < NG:
                    load_exp_rows(sp, n + 1, 1 - par)
                    place_maxima(sp, n + 1, 1 - par, visit + par)

            group(0, 0, 0)
            group(1, 1, 0)
            sp.wait_ge(s["rows_b1"], 16 * (4 + 2 * len(TERMS)))
            with sp.Fori(1, NG // 2 - 1) as i:
                group(2 * i, 0, i)
                group(2 * i + 1, 1, i)
            group(NG - 2, 0, NG // 2 - 1)
            group(NG - 1, 1, NG // 2 - 1)
            for c in range(NCH):
                sp.wait_ge(s["out_ready"], c + 1)
                sp.dma_start(out_tiles[:, 4 * c:4 * c + 4, :], res[:, 4 * c:4 * c + 4, :])\
                    .then_inc(s["out_stored"], 16)
            sp.wait_ge(s["out_stored"], 16 * NCH)

        v_view = v_all[:].rearrange("p (n k h w) -> p n k h w", n=NG, k=NB, h=2)

        @block.gpsimd
        def _(pool):
            pool.memset(identf[:], 0.0).then_inc(s["ident"], 1)
            pool.memset(identb[:], 0.0).then_inc(s["ident"], 1)
            pool.memset(mask_zero[:], 0.0).then_inc(s["ident"], 1)
            pool.memset(ones_rows[:], 1.0).then_inc(s["ones_set"], 1)
            pool.wait_ge(s["ident"], 3)
            for m in (identf, identb):
                pool.affine_select(out=m[:], in_=m[:], compare_op=ALU.not_equal, fill=1.0, base=0,
                                   pattern=[[-1, P]], channel_multiplier=1).then_inc(s["ident"], 1)
            pool.affine_select(out=mask[:], in_=mask_zero[:], compare_op=ALU.is_ge, fill=NEG, base=0,
                               pattern=[[0, 2], [-1, P]], channel_multiplier=1).then_inc(s["mask_set"], 1)
            for i in range(2):
                pool.memset(v_grp[i][:], 0.0).then_inc(s["vpad_set"], 1)
            pool.wait_ge(s["vpad_set"], 2)
            for i in range(2):
                pool.memset(v_grp[i][:, :, :, VW:VW + 1], 1.0).then_inc(s["vpad_set"], 1)
            pool.memset(x1T[:, :, 0:1], 0.0).then_inc(s["xcol_set"], 1)
            pool.memset(minus_half[:], -0.5).then_inc(s["half_set"], 1)
            pool.wait_ge(s["half_set"], 1)
            pool.wait_ge(s["vpad_set"], 4)

            def stage_values(n, par):
                wait(pool, s["summed"], NQ * (n - 1))
                pool.tensor_copy(v_grp[par][:, :, :, 0:VW], v_view[:, n]).then_inc(s["v_grp_set"], 1)

            pool.wait_ge(s["v_copied"], NCH)
            stage_values(0, 0)

            def group(n, par):
                for k in range(NQ):
                    if DIAG[k]:
                        pool.wait_ge(s["exped"], 2 * NQ * n + 2 * k + 2).then_inc(s["quad_seen"], 1)
                    for col in DIAG[k]:
                        e = e_buf[:, k % ESLOTS, :, col:col + P]
                        pool.affine_select(out=e, in_=e, compare_op=ALU.is_ge, fill=0.0, base=0,
                                           pattern=[[0, SUBS], [1, P]], channel_multiplier=-1)\
                            .then_inc(s["masked"], 1)
                    if k == 2 and not (isinstance(n, int) and n + 1 >= NG):
                        stage_values(n + 1, 1 - par)

            group(0, 0)
            group(1, 1)
            with pool.Fori(1, NG // 2 - 1) as i:
                group(2 * i, 0)
                group(2 * i + 1, 1)
            group(NG - 2, 0)
            group(NG - 1, 1)

            pool.wait_ge(s["tail_d"], 7)
            pool.tensor_tensor(rstd[:], ssum[:], minus_half[:], ALU.pow).then_inc(s["rms_rooted"], 1)
            for ve, rs, stats, rooted in ((ve1, rs1, s["stats1"], s["rooted1"]), (ve2, rs2, s["stats2"], s["rooted2"])):
                for ch in range(NCH):
                    pool.wait_ge(stats, 9 * ch + 9)
                    tiles = slice(4 * ch, 4 * ch + 4)
                    pool.tensor_tensor(rs[:, tiles], ve[:, tiles], minus_half[:, tiles], ALU.pow).then_inc(rooted, 1)

        @block.tensor
        def _(pe):
            def max_unit(n, par, k):
                matmuls, diags = MAX_UNITS[k // SUBS]
                j = k % SUBS
                bank = mx[(par + k) % 2]
                if k == 0:
                    wait(pe, s_qkm[par], 32 * (n // 2 + 1) if isinstance(n, int) else 16 * (n - par) + 32)
                if k == 1:
                    wait(pe, s["negmax_copied"], n)
                else:
                    wait(pe, s["maxed"], NU * n + (k - 1 if k >= 2 else 0))
                for i, col in enumerate(diags):
                    pe.matmul(bank[:, col:col + P], identb[:], mask[:, 0, :], start=i == 0, stop=False,
                              skip_group_check=True)
                rows = slice(STRIP * j, STRIP * j + KROWS)
                for i, (col, qb, kb, nk) in enumerate(matmuls):
                    last = pe.matmul(bank[:, col:col + P * nk], qm[par][rows, P * qb:P * (qb + 1)],
                                     km[par][rows, P * kb:P * (kb + nk)], start=not diags and i == 0,
                                     stop=i == len(matmuls) - 1, skip_group_check=True)
                last.then_inc(s["max_scored"], 1)

            def turn_maxima(n, par):
                pe.wait_ge(s["negmax_done"], n + 1)
                turned = mx[(par + NU) % 2][:].bitcast(BF16)
                for qb in range(NB):
                    last = pe.transpose(turned[0:2 * SUBS, P * qb:P * (qb + 1)],
                                        neg_max[:].rearrange("p e j q -> p q (e j)")[:, qb, :], identb[:])
                last.then_inc(s["negmax_turned"], 1)

            def score_pair(n, par, k, p):
                if k == 0 and p == 0:
                    wait(pe, s_qke[par], 32 * (n // 2 + 1) if isinstance(n, int) else 16 * (n - par) + 32)
                    pe.wait_ge(s["max_rows_in"], 32 * n + 32)
                wait(pe, s["exped"], 2 * NQ * n + 2 * (k - 1) + p + 1)
                c, blocks = QUADS[k]
                for jj in range(2):
                    j = 2 * p + jj
                    rows = slice(STRIP * j, STRIP * j + XROWS)
                    for kb, col, w in blocks:
                        q1 = BANK * (c + 1)
                        last = pe.matmul(ex[p][:, jj, col:col + w], ke[par][rows, P * kb:P * (kb + 1)],
                                         qe[par][rows, q1 - w:q1], start=True, stop=True)
                last.then_inc(s["scored"], 1)

            def sum_quad(n, par, k):
                c, blocks = QUADS[k]
                if k == 0:
                    pe.wait_ge(s["v_grp_set"], n + 1)
                if k in (0, 3):
                    wait(pe, s["o_stored"], 2 * n + c - 1)
                pe.wait_ge(s["exped"], 2 * NQ * n + 2 * k + 2)
                if DIAG[k]:
                    pe.wait_ge(s["masked"], NSEL * n + SEL_BY[k])
                for kb, col, w in blocks:
                    for j in range(SUBS):
                        last = pe.matmul(acc[c][STRIP * j:STRIP * (j + 1), BANK - w:BANK],
                                         v_grp[par][:, kb, j // 2, :],
                                         e_buf[:, k % ESLOTS, j, col:col + w],
                                         start=k in (0, 3), stop=k in (2, NQ - 1), skip_group_check=True)
                last.then_inc(s["summed"], 1)

            def turn_sums(n, c):
                pe.wait_ge(s["acc_copied"], 2 * n + c + 1)
                for qb in range(4):
                    last = pe.transpose(acc[c][:, P * qb:P * (qb + 1)], o_rows[c][:, P * qb:P * (qb + 1)],
                                        identf[:])
                last.then_inc(s["acc_turned"], 1)

            pe.wait_ge(s["ident"], 5)
            pe.wait_ge(s["x_in"], 16)
            for t in range(NT):
                last = pe.transpose(wide[t // 4][:, P * (t % 4):P * (t % 4 + 1)], x_tok[:, t, :], identf[:])
                if t % 4 == 3:
                    last.then_inc(s["xt_done"], 1)
            pe.wait_ge(s["wqk_in"], 32)
            for ch in range(NCH):
                if ch % 2 == 0:
                    pe.wait_ge(s["xt_copied_a"], ch // 2 + 1)
                else:
                    pe.wait_ge(s["xt_copied_d"], ch // 2 + 1)
                for w, weights in enumerate((wq_sb, wk_sb)):
                    m = 2 * ch + w
                    wait(pe, s["rest_done"], m - 3)
                    pe.matmul(narrow[m % 4], weights[:], xT[:, BANK * ch:BANK * (ch + 1)], start=True,
                              stop=True).then_inc(s["proj_done"], 1)
            pe.wait_ge(s["wv_in"], 16)
            for t in range(NT):
                last = pe.matmul(wide[t // 4][:, P * (t % 4):P * (t % 4 + 1)], xT[:, P * t:P * (t + 1)],
                                 wv_sb[:], start=True, stop=True)
                if t % 4 == 3:
                    last.then_inc(s["v_done"], 1)
            pe.wait_ge(s["w_in"], 16 * 4)
            pe.wait_ge(s["v_copied"], NCH)
            for i in range(3):
                last = pe.transpose(wide[0][:, P * i:P * (i + 1)], wf_sb[:, i, :], identf[:])
            last.then_inc(s["wt_done"], 1)

            pe.wait_ge(s["mask_set"], 1)
            pe.wait_ge(s["rest_done"], 2 * NCH)
            for k in range(NU):
                max_unit(0, 0, k)
            turn_maxima(0, 0)
            for k in range(EARLY):
                max_unit(1, 1, k)
            pe.wait_ge(s["wvt_copied"], 1)
            pe.wait_ge(s["wt_scaled"], 4)

            def group(n, par):
                static = isinstance(n, int)
                for k in range(NQ):
                    if k < TQUAD:
                        units = [] if static and n + 1 >= NG else \
                            [(n + 1, 1 - par, EARLY + sum(UNITS_AT[:k]) + u) for u in range(UNITS_AT[k])]
                    else:
                        units = [] if static and n + 2 >= NG else \
                            [(n + 2, par, sum(UNITS_AT[TQUAD:k]) + u) for u in range(UNITS_AT[k])]
                    score_pair(n, par, k, 0)
                    if k == TQUAD and not (static and n + 1 >= NG):
                        turn_maxima(n + 1, 1 - par)
                    for u in units[:1]:
                        max_unit(*u)
                    score_pair(n, par, k, 1)
                    for u in units[1:2]:
                        max_unit(*u)
                    if k == 0:
                        if not (static and n == 0):
                            sum_quad(n - 1, 1 - par, NQ - 1)
                    else:
                        sum_quad(n, par, k - 1)
                    if k == 1 and not (static and n == 0):
                        turn_sums(n - 1, 1)
                    if k == 4:
                        turn_sums(n, 0)
                    for u in units[2:]:
                        max_unit(*u)

            group(0, 0)
            group(1, 1)
            with pe.Fori(1, NG // 2 - 1) as i:
                group(2 * i, 0)
                group(2 * i + 1, 1)
            group(NG - 2, 0)
            group(NG - 1, 1)
            sum_quad(NG - 1, 1, NQ - 1)
            turn_sums(NG - 1, 1)

            attn_tiles = reuse(8192, NT * P, "p (t e) -> p t e", t=NT)
            pe.wait_ge(s["attn_ready"], 1)
            for ch in range(NCH):
                for i in range(4):
                    t = 4 * ch + i
                    last = pe.transpose(wide[ch][:, P * i:P * (i + 1)], attn_tiles[:, t, :],
                                        identf[:])
                last.then_inc(s["a_turned"], 1)
            pe.wait_ge(s["rms_done"], 2)
            for ch in range(NCH):
                pe.wait_ge(s["a_copied"], ch + 1)
                if ch == 0:
                    pe.wait_ge(s["o_stored"], 2 * NG)
                for i in range(4):
                    last = pe.matmul(narrow[ch][:, P * i:P * (i + 1)], attnT[:, ch, P * i:P * (i + 1)],
                                     wo_scaled[:], start=True, stop=True)
                last.then_inc(s["a_projected"], 1)
            for ch in range(NCH):
                pe.wait_ge(s["x1_ready"], ch + 1)
                for i in range(4):
                    last = pe.transpose(wide[ch][:, P * i:P * (i + 1)], x1[:, 4 * ch + i, :], identf[:])
                last.then_inc(s["x1_turned"], 1)
            pe.wait_ge(s["xcol_set"], 1)
            for ch in range(NCH):
                b, t0 = ch * BANK // S, ch * BANK % S
                pe.wait_ge(s["x1_copied"], ch + 1)
                pe.wait_ge(s["y_added"], ch + 1)
                pe.matmul(narrow[ch], w_cur[:, 1, :], x1T[:, b, 1 + t0:1 + t0 + BANK], start=True, stop=False)
                pe.matmul(narrow[ch], w_prev[:, 1, :], x1T[:, b, t0:t0 + BANK], start=False, stop=True)\
                    .then_inc(s["k_scored"], 1)
                for i in range(4):
                    o = wide[ch][:, P * i:P * (i + 1)]
                    t1 = t0 + P * i
                    pe.matmul(o, x1T[:, b, 1 + t1:1 + t1 + P], w_cur[:, 0, :], start=True, stop=False)
                    last = pe.matmul(o, x1T[:, b, t1:t1 + P], w_prev[:, 0, :], start=False, stop=True)
                last.then_inc(s["r_scored"], 1)
            for ch in range(NCH):
                pe.wait_ge(s["k_squared"], ch + 1)
                for i in range(4):
                    last = pe.matmul(narrow[ch][:, P * i:P * (i + 1)], k_act[:, ch, P * i:P * (i + 1)], wvT[:],
                                     start=True, stop=True)
                last.then_inc(s["o_scored"], 1)

        o_view = o_tok[:].rearrange("p (n c q j w) -> p n c q j w", n=NG, c=2, q=4, j=SUBS)

        @block.scalar
        def _(act):
            act.dma_start(wo_sb[:], Wo).then_inc(s["w_in"], 16)
            for i, w in enumerate((W_r, W_k, W_v)):
                act.dma_start(wf_sb[:, i, :], w).then_inc(s["w_in"], 16)
            for i, m in enumerate((mu_r, mu_k)):
                act.dma_start(mu[:, i:i + 1], m.unsqueeze(1)).then_inc(s["small_in"], 16)
            for i, l in enumerate((lq1, lq2, lk1, lk2)):
                act.dma_start(lam_in[:, i, :], l.partition_broadcast(P)).then_inc(s["small_in"], 16)
            act.dma_start(w_bounce, rms_w.partition_broadcast(HEADS)).then_inc(s["bounce_in"], 16)
            act.wait_ge(s["bounce_in"], 16)
            act.dma_start(rms_col[:], w_bounce.rearrange("h w -> (h w)").unsqueeze(1)).then_inc(s["small_in"], 16)

            for ch in range(0, NCH, 2):
                act.wait_ge(s["xt_done"], ch + 1)
                nc.scalar.copy(xT[:, BANK * ch:BANK * (ch + 1)], wide[ch]).then_inc(s["xt_copied_a"], 1)

            def high(m):
                act.wait_ge(s["proj_done"], m + 1)
                nc.scalar.activation(parts[m % 2][0][:].rearrange("p b t -> p (b t)")[:, BANK * (m // 2):BANK * (m // 2 + 1)],
                                     narrow[m % 4], ACT.Copy, scale=SCALE if m % 2 == 0 else 1.0)\
                    .then_inc(s["hi_done"], 1)

            def middle(m):
                act.wait_ge(s["rest_done"], m + 1)
                nc.scalar.copy(parts[m % 2][1][:].rearrange("p b t -> p (b t)")[:, BANK * (m // 2):BANK * (m // 2 + 1)],
                               rest[:, m % 4, :]).then_inc(s["mid_done"], 1)

            high(0)
            for m in range(1, 2 * NCH):
                high(m)
                middle(m - 1)
            middle(2 * NCH - 1)
            act.wait_ge(s["lam_dots"], 2)
            nc.scalar.activation(lam_exp[:], lam_sum[:], ACT.Exp).then_inc(s["lam_exped"], 1)
            act.wait_ge(s["wt_done"], 1)
            nc.scalar.copy(wvT[:], wide[0][:, 2 * P:3 * P]).then_inc(s["wvt_copied"], 1)

            def copy_maxima(n, par):
                wait(act, s["max_rows_in"], 32 * n)
                act.wait_ge(s["negmax_turned"], n + 1)
                nc.scalar.copy(max_rows[:], mx[(par + NU) % 2][0:2 * SUBS, :].bitcast(BF16))\
                    .then_inc(s["negmax_copied"], 1)

            def take_sums(n, c):
                act.wait_ge(s["summed"], NQ * n + (3 if c == 0 else NQ))
                wait(act, s["acc_turned"], 2 * n + c - 1)
                nc.scalar.copy(o_rows[c][:], acc[c][:]).then_inc(s["acc_copied"], 1)

            def store_sums(n, c):
                act.wait_ge(s["acc_turned"], 2 * n + c + 1)
                nc.scalar.copy(o_view[:, n, c],
                               acc[c][:].rearrange("p (q j w) -> p q j w", q=4, j=SUBS)[:, :, :, 0:VW + 1])\
                    .then_inc(s["o_stored"], 1)

            copy_maxima(0, 0)

            def group(n, par):
                static = isinstance(n, int)
                for k in range(NQ):
                    used = max(col + w for _, col, w in QUADS[k][1])
                    for p in range(2):
                        act.wait_ge(s["scored"], 2 * NQ * n + 2 * k + p + 1)
                        if p == 0:
                            wait(act, s["summed"], NQ * n + k - ESLOTS + 1)
                        nc.scalar.activation(e_buf[:, k % ESLOTS, 2 * p:2 * p + 2, 0:used], ex[p][:, :, 0:used],
                                             ACT.Exp).then_inc(s["exped"], 1)
                    if k == 0 and not (static and n == 0):
                        take_sums(n - 1, 1)
                    if k == 2 and not (static and n == 0):
                        store_sums(n - 1, 1)
                    if k == 3:
                        take_sums(n, 0)
                    if k == 5:
                        store_sums(n, 0)
                    if k == TQUAD and not (static and n + 1 >= NG):
                        copy_maxima(n + 1, 1 - par)

            group(0, 0)
            group(1, 1)
            with act.Fori(1, NG // 2 - 1) as i:
                group(2 * i, 0)
                group(2 * i + 1, 1)
            group(NG - 2, 0)
            group(NG - 1, 1)
            take_sums(NG - 1, 1)
            store_sums(NG - 1, 1)

            for ch in range(NCH):
                act.wait_ge(s["a_turned"], ch + 1)
                nc.scalar.copy(attnT[:, ch, :], wide[ch]).then_inc(s["a_copied"], 1)
            for ch in range(NCH):
                b, t0 = ch * BANK // S, ch * BANK % S
                act.wait_ge(s["x1_turned"], ch + 1)
                nc.scalar.copy(x1T[:, b, 1 + t0:1 + t0 + BANK], wide[ch]).then_inc(s["x1_copied"], 1)
            for ch in range(NCH):
                act.wait_ge(s["k_scored"], ch + 1)
                nc.scalar.activation(k_relu[:, ch, :], narrow[ch], ACT.Relu).then_inc(s["k_relued"], 1)
                act.wait_ge(s["r_scored"], ch + 1)
                nc.scalar.activation(r_exp[:, ch, :], wide[ch], ACT.Exp, scale=-1.0).then_inc(s["r_exped"], 1)

        @block.vector
        def _(dve):
            for ch in range(1, NCH, 2):
                dve.wait_ge(s["xt_done"], ch + 1)
                nc.vector.tensor_copy(xT[:, BANK * ch:BANK * (ch + 1)], wide[ch]).then_inc(s["xt_copied_d"], 1)

            def remainder(m):
                dve.wait_ge(s["hi_done"], m + 1)
                wait(dve, s["lo_done"], m - 3)
                hi = parts[m % 2][0][:].rearrange("p b t -> p (b t)")[:, BANK * (m // 2):BANK * (m // 2 + 1)]
                nc.vector.scalar_tensor_tensor(out=rest[:, m % 4, :], in0=narrow[m % 4],
                                               scalar=SCALE if m % 2 == 0 else 1.0, in1=hi, op0=ALU.mult,
                                               op1=ALU.subtract).then_inc(s["rest_done"], 1)

            def low(m):
                dve.wait_ge(s["mid_done"], m + 1)
                cols = slice(BANK * (m // 2), BANK * (m // 2 + 1))
                mid, lo = (parts[m % 2][a][:].rearrange("p b t -> p (b t)")[:, cols] for a in (1, 2))
                nc.vector.tensor_tensor(lo, rest[:, m % 4, :], mid, ALU.subtract).then_inc(s["lo_done"], 1)

            remainder(0)
            for m in range(1, 2 * NCH):
                remainder(m)
                low(m - 1)
            low(2 * NCH - 1)
            for ch in range(NCH):
                b, kb = ch // 2, ch % 2 * 4
                dve.wait_ge(s["v_done"], ch + 1)
                src = wide[ch].rearrange("p (k g w) -> p k g w", k=4, g=GPB)
                dst = v_all[:].rearrange("p (b g k w) -> p b k g w", b=B, g=GPB, k=NB)[:, b, kb:kb + 4]
                nc.vector.tensor_copy(dst, src).then_inc(s["v_copied"], 1)
            dve.wait_ge(s["small_in"], 16 * 7)
            nc.vector.tensor_tensor(lam_prod[:], lam_in[:, 0:2, :], lam_in[:, 2:4, :], ALU.mult)\
                .then_inc(s["lam_dots"], 1)
            dve.wait_ge(s["lam_dots"], 1)
            nc.vector.tensor_reduce(lam_sum[:], lam_prod[:], AX.X, ALU.add).then_inc(s["lam_dots"], 1)
            nc.vector.tensor_scalar(rms_scaled[:], rms_col[:], 1.0 - LAMBDA_INIT, None, ALU.mult)\
                .then_inc(s["rms_done"], 1)
            nc.vector.tensor_scalar(mu1[:], mu[:], -1.0, 1.0, ALU.mult, ALU.add).then_inc(s["wt_scaled"], 1)
            dve.wait_ge(s["rms_done"], 1)
            dve.wait_ge(s["w_in"], 16 * 4)
            nc.vector.tensor_scalar(wo_scaled[:], wo_sb[:], rms_scaled[:], None, ALU.mult).then_inc(s["rms_done"], 1)
            dve.wait_ge(s["lam_exped"], 1)
            nc.vector.scalar_tensor_tensor(out=lam_neg[:], in0=lam_exp[:, 1:2], scalar=-LAMBDA_INIT,
                                           in1=lam_exp[:, 0:1], op0=ALU.add, op1=ALU.subtract)\
                .then_inc(s["lam_done"], 1)
            dve.wait_ge(s["wt_done"], 1)
            dve.wait_ge(s["wvt_copied"], 1)
            dve.wait_ge(s["wt_scaled"], 1)
            for i in range(2):
                src = wide[0][:, P * i:P * (i + 1)]
                nc.vector.tensor_scalar(w_cur[:, i, :], src, mu[:, i:i + 1], None, ALU.mult)
                nc.vector.tensor_scalar(w_prev[:, i, :], src, mu1[:, i:i + 1], None, ALU.mult)\
                    .then_inc(s["wt_scaled"], 1)
            dve.wait_ge(s["wt_scaled"], 3)
            nc.vector.memset(far_max[:], 0.0).then_inc(s["wt_scaled"], 1)

            def max_unit(n, par, k):
                dve.wait_ge(s["max_scored"], NU * n + k + 1)
                u, j = divmod(k, SUBS)
                if k == 0:
                    wait(dve, s["combined"], 5 * n)
                nc.vector.tensor_reduce(part_max[:, j, u, :],
                                        mx[(par + k) % 2][:].rearrange("p (a b) -> p a b", a=4), AX.X, ALU.max)\
                    .then_inc(s["maxed"], 1)

            def combine(n):
                dve.wait_ge(s["maxed"], NU * (n + 1))
                wait(dve, s["negmax_done"], n)
                wait(dve, s["negmax_turned"], n)
                nc.vector.tensor_reduce(row_max[:, :, 2:8:4], part_max[:, :, 0:2, 1:4], AX.X, ALU.max)\
                    .then_inc(s["combined"], 1)
                nc.vector.tensor_reduce(row_max[:, :, 3:8:4], part_max[:, :, 2:4, :], AX.X, ALU.max)\
                    .then_inc(s["combined"], 1)
                nc.vector.tensor_reduce(row_max[:, :, 1:8:4],
                                        part_max[:, :, 8, :].rearrange("p j (a b) -> p j a b", a=2),
                                        AX.X, ALU.max).then_inc(s["combined"], 1)
                nc.vector.tensor_copy(row_max[:, :, 0:8:4], part_max[:, :, 0:2, 0]).then_inc(s["combined"], 1)
                nc.vector.tensor_reduce(far_max[:], part_max[:, :, 4:8, :], AX.X, ALU.max)\
                    .then_inc(s["combined"], 1)
                dve.wait_ge(s["combined"], 5 * n + 5)
                nc.vector.tensor_tensor(row_max[:, :, 4:8], row_max[:, :, 4:8], far_max[:], ALU.max)\
                    .then_inc(s["normed_d"], 1)
                dve.wait_ge(s["normed_d"], 2 * n + 1)
                nc.vector.tensor_scalar(neg_max[:, 0], row_max[:], -1.0, None, ALU.mult).then_inc(s["normed_d"], 1)
                dve.wait_ge(s["normed_d"], 2 * n + 2)
                nc.vector.scalar_tensor_tensor(out=neg_max[:, 1], in0=row_max[:], scalar=-1.0,
                                               in1=neg_max[:, 0], op0=ALU.mult, op1=ALU.subtract)\
                    .then_inc(s["negmax_done"], 1)

            for k in range(NU):
                max_unit(0, 0, k)
            combine(0)
            for k in range(EARLY):
                max_unit(1, 1, k)

            def group(n, par):
                static = isinstance(n, int)
                if not (static and n + 1 >= NG):
                    for k in range(EARLY, NU):
                        max_unit(n + 1, 1 - par, k)
                    combine(n + 1)
                if not (static and n + 2 >= NG):
                    for k in range(EARLY):
                        max_unit(n + 2, par, k)

            group(0, 0)
            group(1, 1)
            with dve.Fori(1, NG // 2 - 1) as i:
                group(2 * i, 0)
                group(2 * i + 1, 1)
            group(NG - 2, 0)

            sums = o_tok[:].rearrange("p (m j w) -> p m j w", j=SUBS, w=VW + 1)
            dve.wait_ge(s["o_stored"], 2 * NG)
            nc.vector.reciprocal(r_den[:], sums[:, :, :, VW]).then_inc(s["tail_d"], 1)
            dve.wait_ge(s["tail_d"], 1)
            dve.wait_ge(s["lam_done"], 1)
            nc.vector.tensor_scalar(r_den[:, :, 1::2], r_den[:, :, 1::2], lam_neg[:], None, ALU.mult)\
                .then_inc(s["tail_d"], 1)
            dve.wait_ge(s["tail_d"], 2)
            rd = r_den[:].rearrange("p m j -> p (m j)").unsqueeze(2).broadcast_to([P, NG * NB * SUBS, VW])
            nc.vector.tensor_tensor(o_scaled.rearrange("p m j w -> p (m j) w"),
                                    sums[:, :, :, 0:VW].rearrange("p m j w -> p (m j) w"), rd, ALU.mult)\
                .then_inc(s["tail_d"], 1)
            dve.wait_ge(s["tail_d"], 3)
            nc.vector.tensor_tensor(attn, o_scaled[:, :, 0::2, :], o_scaled[:, :, 1::2, :], ALU.add)\
                .then_inc(s["tail_d"], 1)
            dve.wait_ge(s["tail_d"], 4)
            nc.vector.tensor_tensor(attn_sq, attn, attn, ALU.mult).then_inc(s["tail_d"], 1)
            dve.wait_ge(s["tail_d"], 5)
            nc.vector.tensor_reduce(ssum[:], attn_sq.rearrange("p m h w -> p (m h) w"), AX.X, ALU.add)\
                .then_inc(s["tail_d"], 1)
            dve.wait_ge(s["tail_d"], 6)
            nc.vector.tensor_scalar(ssum[:], ssum[:], 1.0 / VW, RMS_EPS, ALU.mult, ALU.add)\
                .then_inc(s["tail_d"], 1)
            dve.wait_ge(s["tail_d"], 7)
            dve.wait_ge(s["rms_rooted"], 1)
            for b in range(B):
                ms = slice(b * GPB * NB, (b + 1) * GPB * NB)
                rs = rstd[:].rearrange("p (b g q h) -> p b g q h", b=B, g=GPB, h=2)[:, b]
                last = nc.vector.tensor_tensor(attn_n[:, b], attn[:, ms].rearrange("p (g q) h w -> p g q h w", g=GPB),
                                               rs.unsqueeze(4).broadcast_to([P, GPB, NB, 2, VW]), ALU.mult)
            last.then_inc(s["attn_ready"], 1)

            def layer_norm(src, st, mv, ve, rs, dst, ch, stats, rooted, ready):
                for i in range(4):
                    nc.vector.bn_stats(st[:, 4 * ch + i, :], src[:, 4 * ch + i, :]).then_inc(stats, 1)
                dve.wait_ge(stats, 9 * ch + 4)
                for i in range(4):
                    nc.vector.bn_aggr(mv[:, 4 * ch + i, :], st[:, 4 * ch + i, :]).then_inc(stats, 1)
                dve.wait_ge(stats, 9 * ch + 8)
                nc.vector.tensor_scalar(ve[:, 4 * ch:4 * ch + 4], mv[:, 4 * ch:4 * ch + 4, 1], LN_EPS, None,
                                        ALU.add).then_inc(stats, 1)
                dve.wait_ge(rooted, ch + 1)
                for i in range(4):
                    t = 4 * ch + i
                    last = nc.vector.tensor_scalar(dst[:, t, :], src[:, t, :], mv[:, t, 0:1], rs[:, t:t + 1],
                                                   ALU.subtract, ALU.mult)
                last.then_inc(ready, 1)

            for ch in range(NCH):
                dve.wait_ge(s["a_projected"], ch + 1)
                nc.vector.tensor_tensor(y[:, 4 * ch:4 * ch + 4, :], narrow[ch].rearrange("p (t c) -> p t c", t=4),
                                        x_tok[:, 4 * ch:4 * ch + 4, :], ALU.add).then_inc(s["y_added"], 1)
                dve.wait_ge(s["y_added"], ch + 1)
                layer_norm(y, st1, mv1, ve1, rs1, x1, ch, s["stats1"], s["rooted1"], s["x1_ready"])
            for ch in range(NCH):
                dve.wait_ge(s["k_relued"], ch + 1)
                nc.vector.tensor_tensor(k_act[:, ch, :], k_relu[:, ch, :], k_relu[:, ch, :], ALU.mult)\
                    .then_inc(s["k_squared"], 1)
            for ch in range(NCH):
                dve.wait_ge(s["r_exped"], ch + 1)
                nc.vector.tensor_scalar(r_one[:, ch, :], r_exp[:, ch, :], 1.0, None, ALU.add)\
                    .then_inc(s["z_steps"], 1)
                dve.wait_ge(s["z_steps"], 3 * ch + 1)
                nc.vector.reciprocal(r_sig[:, ch, :], r_one[:, ch, :]).then_inc(s["z_steps"], 1)
                dve.wait_ge(s["z_steps"], 3 * ch + 2)
                dve.wait_ge(s["o_scored"], ch + 1)
                nc.vector.tensor_tensor(z0[:, ch, :], narrow[ch], r_sig[:, ch, :], ALU.mult)\
                    .then_inc(s["z_steps"], 1)
                dve.wait_ge(s["z_steps"], 3 * ch + 3)
                nc.vector.tensor_tensor(z[:, 4 * ch:4 * ch + 4, :], z0[:, ch, :].rearrange("p (t c) -> p t c", t=4),
                                        x1[:, 4 * ch:4 * ch + 4, :], ALU.add).then_inc(s["z_ready"], 1)
                dve.wait_ge(s["z_ready"], ch + 1)
                layer_norm(z, st2, mv2, ve2, rs2, res, ch, s["stats2"], s["rooted2"], s["out_ready"])


_INS = ["L0_attn_x", "L0_attn_Wq", "L0_attn_Wk", "L0_attn_Wv", "L0_attn_Wo", "L0_attn_lq1", "L0_attn_lk1",
        "L0_attn_lq2", "L0_attn_lk2", "L0_attn_rms_w", "L0_ffn_W_r", "L0_ffn_W_k", "L0_ffn_W_v",
        "L0_ffn_mu_r", "L0_ffn_mu_k"]


def kernel(**inputs):
    import numpy as _np
    import concourse.bacc as _bacc
    from concourse import mybir as _mybir
    from concourse.bass_utils import run_bass_kernel_spmd as _run

    nc = _bacc.Bacc("TRN2", target_bir_lowering=False, num_devices=1)
    arrays, args = {}, []
    for name in _INS:
        a = _np.ascontiguousarray(inputs[name])
        arrays[f"in_{name}"] = a
        args.append(nc.dram_tensor(f"in_{name}", a.shape, _mybir.dt.from_np(a.dtype), kind="ExternalInput").ap())
    shape = inputs["L0_attn_x"].shape
    args.append(nc.dram_tensor("out_0", shape, _mybir.dt.float32, kind="ExternalOutput").ap())
    build(nc, *args)
    r = _run(nc, [arrays], core_ids=[0])
    return r.results[0]["out_0"]
```

```python
import math
from contextlib import ExitStack

import concourse.bass as bass
from concourse import mybir

F32 = mybir.dt.float32
BF16 = mybir.dt.bfloat16
ALU = mybir.AluOpType
ACT = mybir.ActivationFunctionType
AX = mybir.AxisListType

P = 128
BANK = 512
HEADS = 16
D = P // HEADS // 2
VW = 2 * D
SUBS = 4
STRIP = 32
LAMBDA_INIT = 0.8 - 0.6 * math.exp(-0.3 * 12)
RMS_EPS = 1e-5
LN_EPS = 1e-5
NEG = -1e30

TERMS = [(0, 0), (0, 1), (1, 0), (1, 1), (0, 2), (2, 0)]
KROWS = len(TERMS) * D
XROWS = KROWS + 2

MAX_UNITS = [
    ([(0, 0, 0, 1), (128, 2, 0, 3)], [0, 384]),
    ([(0, 4, 4, 1), (128, 6, 4, 3)], [0, 384]),
    ([(0, 3, 0, 4)], [384]),
    ([(0, 7, 4, 4)], [384]),
    ([(0, 4, 0, 4)], []),
    ([(0, 5, 0, 4)], []),
    ([(0, 6, 0, 4)], []),
    ([(0, 7, 0, 4)], []),
    ([(0, 1, 0, 2), (256, 5, 4, 2)], [128, 384]),
]
NU = len(MAX_UNITS) * SUBS
RING = NU + 1

QUADS = [
    (0, [(0, 0, 512)]),
    (0, [(1, 0, 384), (3, 384, 128)]),
    (0, [(2, 0, 256)]),
    (1, [(0, 0, 512)]),
    (1, [(1, 0, 512)]),
    (1, [(2, 0, 512)]),
    (1, [(3, 0, 512)]),
    (1, [(4, 0, 512)]),
    (1, [(5, 0, 384), (7, 384, 128)]),
    (1, [(6, 0, 256)]),
]
NQ = len(QUADS)
ESLOTS = 5
DIAG = [[col for kb, col, w in parts if kb // 4 == c] for c, parts in QUADS]
NSEL = sum(map(len, DIAG))
SEL_BY = [sum(map(len, DIAG[: k + 1])) for k in range(NQ)]

EARLY = 10
TQUAD = 7
UNITS_AT = [4, 4, 2, 4, 4, 4, 4, 4, 4, 2]
assert sum(UNITS_AT[:TQUAD]) == NU - EARLY and sum(UNITS_AT[TQUAD:]) == EARLY


def wait(eng, sem, value):
    if isinstance(value, int) and value <= 0:
        return
    eng.wait_ge(sem, value)


def build(nc, x, Wq, Wk, Wv, Wo, lq1, lk1, lq2, lk2, rms_w, W_r, W_k, W_v, mu_r, mu_k, out):
    B, S, _ = x.shape
    NB = S // P
    NT = B * NB
    NCH = NT * P // BANK
    GPB = 2 * HEADS // SUBS
    NG = B * GPB
    NSUB = NG * SUBS
    SCALE = D ** -0.5

    q_rows = nc.dram_tensor("q_rows", (NSUB, STRIP, S), BF16, kind="Internal").ap()
    k_rows = nc.dram_tensor("k_rows", (NSUB, STRIP, S), BF16, kind="Internal").ap()
    w_bounce = nc.dram_tensor("w_bounce", (HEADS, VW), F32, kind="Internal").ap()
    q_group = q_rows.rearrange("(n j) r t -> n (j r) t", j=SUBS)
    k_group = k_rows.rearrange("(n j) r t -> n (j r) t", j=SUBS)
    q_subs = q_rows.rearrange("(n j) r t -> n j r t", j=SUBS)
    k_subs = k_rows.rearrange("(n j) r t -> n j r t", j=SUBS)
    LOADS = 16 * (SUBS + 1)
    x_tiles = x.rearrange("b (n p) c -> p (b n) c", p=P)
    out_tiles = out.rearrange("b (n p) c -> p (b n) c", p=P)

    with ExitStack() as ctx:
        def sb(name, shape, dt=F32):
            return ctx.enter_context(nc.sbuf_tensor(name, shape, dt))

        def sem(name):
            return ctx.enter_context(nc.semaphore(name))

        x_tok = sb("x_tok", [P, NT, P])
        xT = sb("xT", [P, NT * P])
        wq_sb, wk_sb, wv_sb, wo_sb = (sb(n, [P, P]) for n in ("wq_sb", "wk_sb", "wv_sb", "wo_sb"))
        wf_sb = sb("wf_sb", [P, 3, P])
        wo_scaled = sb("wo_scaled", [P, P])
        w_cur = sb("w_cur", [P, 2, P])
        w_prev = sb("w_prev", [P, 2, P])
        wvT = sb("wvT", [P, P])
        mu = sb("mu", [P, 2])
        mu1 = sb("mu1", [P, 2])
        rms_col = sb("rms_col", [P, 1])
        rms_scaled = sb("rms_scaled", [P, 1])
        lam_in = sb("lam_in", [P, 4, D])
        lam_prod = sb("lam_prod", [P, 2, D])
        lam_sum = sb("lam_sum", [P, 2])
        lam_exp = sb("lam_exp", [P, 2])
        lam_neg = sb("lam_neg", [P, 1])
        identf = sb("identf", [P, P])
        identb = sb("identb", [P, P], BF16)
        ones_rows = sb("ones_rows", [P, S], BF16)
        zero_rows = sb("zero_rows", [P, S], BF16)
        mask_zero = sb("mask_zero", [P, 2, P], BF16)
        mask = sb("mask", [P, 2, P], BF16)
        parts = [[sb(f"part_{w}{a}", [P, B, S], BF16) for a in range(3)] for w in "qk"]
        rest = sb("rest", [P, 4, BANK])
        v_all = sb("v_all", [P, NG * NB * 2 * VW])
        v_grp = [sb(f"v_grp{i}", [P, NB, 2, STRIP]) for i in range(2)]
        qm = [sb(f"qm{i}", [P, SUBS, S], BF16) for i in range(2)]
        km = [sb(f"km{i}", [P, S], BF16) for i in range(2)]
        qe = [sb(f"qe{i}", [P, S], BF16) for i in range(2)]
        ke = [sb(f"ke{i}", [P, SUBS, S], BF16) for i in range(2)]
        part_max = sb("part_max", [P, SUBS, len(MAX_UNITS), 4])
        far_max = sb("far_max", [P, SUBS, 4])
        row_max = sb("row_max", [P, SUBS, NB])
        neg_max = sb("neg_max", [P, 2, SUBS, NB], BF16)
        max_rows = sb("max_rows", [2 * SUBS, S], BF16)
        e_buf = sb("e_buf", [P, ESLOTS, SUBS, BANK])
        o_rows = [sb(f"o_rows{c}", [P, BANK]) for c in range(2)]
        o_tok = [sb(f"o_tok{i}", [P, NB, SUBS, VW + 1]) for i in range(2)]
        r_den = [sb(f"r_den{i}", [P, NB * SUBS]) for i in range(2)]
        lam_pair = sb("lam_pair", [P, NB * SUBS])
        r_lam = sb("r_lam", [P, NB * SUBS])
        o_scaled = sb("o_scaled", [P, NB * SUBS, VW])
        attn = sb("attn", [P, NB * 2, VW])
        attn_sq = sb("attn_sq", [P, NB * 2, VW])
        sq4 = sb("sq4", [P, NB * 2, 4])
        sq2 = sb("sq2", [P, NB * 2, 2])
        sq1 = sb("sq1", [P, NB * 2])
        sq_eps = sb("sq_eps", [P, NB * 2])
        r_rms = sb("r_rms", [P, NB * 2])
        eps_tile = sb("eps_tile", [P, NB * 2])
        attn_n = sb("attn_n", [P, NB * NG * 2 * VW])

        ex = [ctx.enter_context(nc.psum_tensor(f"ex{i}", [P, 2, BANK], F32)) for i in range(2)]
        acc = [ctx.enter_context(nc.psum_tensor(f"acc{i}", [P, BANK], F32)) for i in range(2)]
        mx = [ctx.enter_context(nc.psum_tensor(f"mx{i}", [P, BANK], F32)) for i in range(2)]
        wide = [ex[0][:, 0, :], ex[0][:, 1, :], ex[1][:, 0, :], ex[1][:, 1, :]]
        narrow = [acc[0][:], acc[1][:], mx[0][:], mx[1][:]]

        names = """x_in wqk_in wv_in w_in small_in bounce_in
                   ident ones_set mask_set vpad_set xcol_set
                   xt_done xt_copied_a xt_copied_d proj_done hi_done rest_done mid_done lo_done
                   v_done v_copied wt_done wvt_copied wt_scaled lam_dots lam_exped lam_done rms_done
                   rows_b0 rows_b1 qkm_in0 qkm_in1 qke_in0 qke_in1 max_rows_in v_grp_set
                   max_scored maxed combined negmax_done negmax_turned negmax_copied
                   scored exped masked summed acc_copied acc_turned o_stored
                   normed_d attn_ready a_turned a_copied a_projected y_added stats1 x1_ready
                   x1_turned x1_copied k_scored r_scored k_relued r_gated k_squared o_scored z_steps z_ready
                   stats2 rooted1 rooted2 half_set quad_seen stacks_zeroed den_inverted values_seen norm_seen norm_steps lam_paired out_ready out_stored""".split()
        s = {n: sem(n) for n in names}
        s_qkm = [s["qkm_in0"], s["qkm_in1"]]
        s_qke = [s["qke_in0"], s["qke_in1"]]

        flat = e_buf[:].rearrange("p s j t -> p (s j t)")

        def reuse(lo, n, pattern, **sizes):
            return flat[:, lo:lo + n].rearrange(pattern, **sizes)

        z0 = reuse(0, NT * P, "p (c t) -> p c t", c=NCH)
        z = reuse(2048, NT * P, "p (t c) -> p t c", t=NT)
        res = reuse(4096, NT * P, "p (t c) -> p t c", t=NT)
        k_relu = reuse(6144, NT * P, "p (c t) -> p c t", c=NCH)
        k_act = reuse(8192, NT * P, "p (c t) -> p c t", c=NCH)
        y = xT[:].rearrange("p (t c) -> p t c", t=NT)
        attnT = sb("attnT", [P, NCH, BANK])
        st1 = sb("st1", [P, NT, 6])
        mv1 = sb("mv1", [P, NT, 2])
        ve1 = sb("ve1", [P, NT])
        rs1 = sb("rs1", [P, NT])
        x1 = sb("x1", [P, NT, P])
        x1T = sb("x1T", [P, B, 1 + S])
        r_gate = v_all[:].rearrange("p (c t) -> p c t", c=NCH)
        st2 = sb("st2", [P, NT, 6])
        mv2 = sb("mv2", [P, NT, 2])
        ve2 = sb("ve2", [P, NT])
        rs2 = sb("rs2", [P, NT])
        minus_half = sb("minus_half", [P, NB * 2])

        block = ctx.enter_context(nc.Block())

        def load_max_rows(sp, n, par):
            wait(sp, s["max_scored"], NU * (n - 1))
            for j in range(SUBS):
                sp.dma_start(qm[par][STRIP * j:STRIP * (j + 1), j, :], q_subs[n][j]).then_inc(s_qkm[par], 16)
            sp.dma_start(km[par][:], k_group[n]).then_inc(s_qkm[par], 16)

        def load_exp_rows(sp, n, par):
            wait(sp, s["scored"], 2 * NQ * (n - 1))
            sp.dma_start(qe[par][:], q_group[n]).then_inc(s_qke[par], 16)
            for j in range(SUBS):
                sp.dma_start(ke[par][STRIP * j:STRIP * (j + 1), j, :], k_subs[n][j]).then_inc(s_qke[par], 16)

        def place_maxima(sp, n, par, visit):
            wait(sp, s_qke[par], LOADS * (visit + 1))
            wait(sp, s["negmax_copied"], n + 1)
            for e in range(2):
                sp.dma_start(qe[par][KROWS + e:P:STRIP, :], max_rows[SUBS * e:SUBS * (e + 1), :])\
                    .then_inc(s["max_rows_in"], 16)

        @block.sync
        def _(sp):
            sp.dma_start(x_tok[:], x_tiles).then_inc(s["x_in"], 16)
            sp.dma_start(wq_sb[:], Wq).then_inc(s["wqk_in"], 16)
            sp.dma_start(wk_sb[:], Wk).then_inc(s["wqk_in"], 16)
            sp.dma_start(wv_sb[:], Wv).then_inc(s["wv_in"], 16)
            sp.wait_ge(s["ones_set"], 2)
            for b, done in enumerate((s["rows_b0"], s["rows_b1"])):
                subs = slice(b * NSUB // B, (b + 1) * NSUB // B)
                for rows, fill in ((q_rows, zero_rows), (k_rows, ones_rows)):
                    for h in range(2):
                        lo = subs.start + h * P // 8
                        sp.dma_start(rows[lo:lo + P // 8, KROWS:STRIP, :], fill[:]).then_inc(done, 16)
                for part, need in ((0, "hi_done"), (1, "mid_done"), (2, "lo_done")):
                    sp.wait_ge(s[need], 4 * (b + 1))
                    for w, rows in enumerate((q_rows, k_rows)):
                        for t, term in enumerate(TERMS):
                            if term[w] == part:
                                sp.dma_start(rows[subs, D * t:D * (t + 1), :], parts[w][part][:, b, :])\
                                    .then_inc(done, 16)
                if b == 0:
                    sp.wait_ge(done, 16 * (4 + 2 * len(TERMS)))
                    sp.wait_ge(s["stacks_zeroed"], 4)
                    load_max_rows(sp, 0, 0)
                    load_max_rows(sp, 1, 1)
                    load_exp_rows(sp, 0, 0)
            place_maxima(sp, 0, 0, 0)

            def group(n, par, visit):
                if not isinstance(n, int) or n + 2 < NG:
                    load_max_rows(sp, n + 2, par)
                if not isinstance(n, int) or n + 1 < NG:
                    load_exp_rows(sp, n + 1, 1 - par)
                    place_maxima(sp, n + 1, 1 - par, visit + par)

            group(0, 0, 0)
            group(1, 1, 0)
            sp.wait_ge(s["rows_b1"], 16 * (4 + 2 * len(TERMS)))
            with sp.Fori(1, NG // 2 - 1) as i:
                group(2 * i, 0, i)
                group(2 * i + 1, 1, i)
            group(NG - 2, 0, NG // 2 - 1)
            group(NG - 1, 1, NG // 2 - 1)
            for c in range(NCH):
                sp.wait_ge(s["out_ready"], c + 1)
                sp.dma_start(out_tiles[:, 4 * c:4 * c + 4, :], res[:, 4 * c:4 * c + 4, :])\
                    .then_inc(s["out_stored"], 16)
            sp.wait_ge(s["out_stored"], 16 * NCH)

        v_view = v_all[:].rearrange("p (n k h w) -> p n k h w", n=NG, k=NB, h=2)

        @block.gpsimd
        def _(pool):
            pool.memset(identf[:], 0.0).then_inc(s["ident"], 1)
            pool.memset(identb[:], 0.0).then_inc(s["ident"], 1)
            pool.memset(mask_zero[:], 0.0).then_inc(s["ident"], 1)
            pool.memset(ones_rows[:], 1.0).then_inc(s["ones_set"], 1)
            pool.memset(zero_rows[:], 0.0).then_inc(s["ones_set"], 1)
            pool.wait_ge(s["ident"], 3)
            for m in (identf, identb):
                pool.affine_select(out=m[:], in_=m[:], compare_op=ALU.not_equal, fill=1.0, base=0,
                                   pattern=[[-1, P]], channel_multiplier=1).then_inc(s["ident"], 1)
            pool.affine_select(out=mask[:], in_=mask_zero[:], compare_op=ALU.is_ge, fill=NEG, base=0,
                               pattern=[[0, 2], [-1, P]], channel_multiplier=1).then_inc(s["mask_set"], 1)
            for stack in (qm[0], ke[0], qm[1], ke[1]):
                pool.memset(stack[:].bitcast(mybir.dt.uint32), 0).then_inc(s["stacks_zeroed"], 1)
            for i in range(2):
                pool.memset(v_grp[i][:], 0.0).then_inc(s["vpad_set"], 1)
            pool.wait_ge(s["vpad_set"], 2)
            for i in range(2):
                pool.memset(v_grp[i][:, :, :, VW:VW + 1], 1.0).then_inc(s["vpad_set"], 1)
            pool.memset(x1T[:, :, 0:1], 0.0).then_inc(s["xcol_set"], 1)
            pool.memset(minus_half[:], -0.5).then_inc(s["half_set"], 1)
            pool.memset(eps_tile[:], VW * RMS_EPS).then_inc(s["half_set"], 1)
            pool.wait_ge(s["half_set"], 2)
            pool.wait_ge(s["vpad_set"], 4)

            def stage_values(n, par):
                if not isinstance(n, int) or n > 1:
                    pool.wait_ge(s["summed"], NQ * (n - 1)).then_inc(s["values_seen"], 1)
                pool.tensor_copy(v_grp[par][:, :, :, 0:VW], v_view[:, n]).then_inc(s["v_grp_set"], 1)

            pool.wait_ge(s["v_copied"], NCH)
            stage_values(0, 0)
            pool.wait_ge(s["lam_paired"], 2)

            attn_out = attn_n[:].rearrange("p (q n h w) -> p n q h w", q=NB, n=NG, h=2)

            def normalise(n, par):
                steps = 9

                def seen(i):
                    wait(pool, s["norm_steps"], steps * n + i)

                pool.wait_ge(s["den_inverted"], n + 1).then_inc(s["norm_seen"], 1)
                pool.tensor_tensor(r_lam[:], r_den[par][:], lam_pair[:], ALU.mult).then_inc(s["norm_steps"], 1)
                seen(1)
                sums = o_tok[par][:].rearrange("p q j w -> p (q j) w")[:, :, 0:VW]
                pool.tensor_tensor(o_scaled[:], sums, r_lam[:].unsqueeze(2).broadcast_to([P, NB * SUBS, VW]),
                                   ALU.mult).then_inc(s["norm_steps"], 1)
                seen(2)
                pool.tensor_tensor(attn[:], o_scaled[:, 0::2, :], o_scaled[:, 1::2, :], ALU.add)\
                    .then_inc(s["norm_steps"], 1)
                seen(3)
                pool.tensor_tensor(attn_sq[:], attn[:], attn[:], ALU.mult).then_inc(s["norm_steps"], 1)
                seen(4)
                pool.tensor_tensor(sq4[:], attn_sq[:, :, 0:4], attn_sq[:, :, 4:8], ALU.add)\
                    .then_inc(s["norm_steps"], 1)
                seen(5)
                pool.tensor_tensor(sq2[:], sq4[:, :, 0:2], sq4[:, :, 2:4], ALU.add).then_inc(s["norm_steps"], 1)
                seen(6)
                pool.tensor_tensor(sq1[:], sq2[:, :, 0], sq2[:, :, 1], ALU.add).then_inc(s["norm_steps"], 1)
                seen(7)
                pool.tensor_tensor(sq_eps[:], sq1[:], eps_tile[:], ALU.add).then_inc(s["norm_steps"], 1)
                seen(8)
                pool.tensor_tensor(r_rms[:], sq_eps[:], minus_half[:], ALU.pow).then_inc(s["norm_steps"], 1)
                pool.wait_ge(s["norm_steps"], steps * n + 9).then_inc(s["norm_seen"], 1)
                pool.tensor_tensor(attn_out[:, n],
                                   attn[:].rearrange("p (q h) w -> p q h w", h=2),
                                   r_rms[:].rearrange("p (q h) -> p q h", h=2).unsqueeze(3)
                                   .broadcast_to([P, NB, 2, VW]), ALU.mult).then_inc(s["attn_ready"], 1)

            def group(n, par):
                for k in range(NQ):
                    if DIAG[k]:
                        pool.wait_ge(s["exped"], 2 * NQ * n + 2 * k + 2).then_inc(s["quad_seen"], 1)
                    for col in DIAG[k]:
                        e = e_buf[:, k % ESLOTS, :, col:col + P]
                        pool.affine_select(out=e, in_=e, compare_op=ALU.is_ge, fill=0.0, base=0,
                                           pattern=[[0, SUBS], [1, P]], channel_multiplier=-1)\
                            .then_inc(s["masked"], 1)
                    if k == 2 and not (isinstance(n, int) and n + 1 >= NG):
                        stage_values(n + 1, 1 - par)
                    if k == 2 and not (isinstance(n, int) and n == 0):
                        normalise(n - 1, 1 - par)

            group(0, 0)
            group(1, 1)
            with pool.Fori(1, NG // 2 - 1) as i:
                group(2 * i, 0)
                group(2 * i + 1, 1)
            group(NG - 2, 0)
            group(NG - 1, 1)

            normalise(NG - 1, 1)

            for ve, rs, stats, rooted in ((ve1, rs1, s["stats1"], s["rooted1"]), (ve2, rs2, s["stats2"], s["rooted2"])):
                for ch in range(NCH):
                    pool.wait_ge(stats, 9 * ch + 9)
                    tiles = slice(4 * ch, 4 * ch + 4)
                    pool.tensor_tensor(rs[:, tiles], ve[:, tiles], minus_half[:, tiles], ALU.pow).then_inc(rooted, 1)

        @block.tensor
        def _(pe):
            def loaded(n, par):
                return LOADS * (n // 2 + 1) if isinstance(n, int) else LOADS // 2 * (n - par) + LOADS

            def max_unit(n, par, k):
                matmuls, diags = MAX_UNITS[k // SUBS]
                j = k % SUBS
                bank = mx[(par + k) % 2]
                if k == 0:
                    wait(pe, s_qkm[par], loaded(n, par))
                if k == 1:
                    wait(pe, s["negmax_copied"], n)
                else:
                    wait(pe, s["maxed"], NU * n + (k - 1 if k >= 2 else 0))
                for i, col in enumerate(diags):
                    pe.matmul(bank[:, col:col + P], identb[:], mask[:, 0, :], start=i == 0, stop=False,
                              skip_group_check=True)
                for i, (col, qb, kb, nk) in enumerate(matmuls):
                    last = pe.matmul(bank[:, col:col + P * nk], qm[par][:, j, P * qb:P * (qb + 1)],
                                     km[par][:, P * kb:P * (kb + nk)], start=not diags and i == 0,
                                     stop=i == len(matmuls) - 1, skip_group_check=True)
                last.then_inc(s["max_scored"], 1)

            def turn_maxima(n, par):
                pe.wait_ge(s["negmax_done"], n + 1)
                turned = mx[(par + NU) % 2][:].bitcast(BF16)
                for qb in range(NB):
                    last = pe.transpose(turned[0:2 * SUBS, P * qb:P * (qb + 1)],
                                        neg_max[:].rearrange("p e j q -> p q (e j)")[:, qb, :], identb[:])
                last.then_inc(s["negmax_turned"], 1)

            def score_pair(n, par, k, p):
                if k == 0 and p == 0:
                    wait(pe, s_qke[par], loaded(n, par))
                    pe.wait_ge(s["max_rows_in"], 32 * n + 32)
                wait(pe, s["exped"], 2 * NQ * n + 2 * (k - 1) + p + 1)
                c, blocks = QUADS[k]
                for jj in range(2):
                    j = 2 * p + jj
                    for kb, col, w in blocks:
                        q1 = BANK * (c + 1)
                        last = pe.matmul(ex[p][:, jj, col:col + w], ke[par][:, j, P * kb:P * (kb + 1)],
                                         qe[par][:, q1 - w:q1], start=True, stop=True)
                last.then_inc(s["scored"], 1)

            def sum_quad(n, par, k):
                c, blocks = QUADS[k]
                if k == 0:
                    pe.wait_ge(s["v_grp_set"], n + 1)
                if k in (0, 3):
                    wait(pe, s["o_stored"], 2 * n + c - 1)
                pe.wait_ge(s["exped"], 2 * NQ * n + 2 * k + 2)
                if DIAG[k]:
                    pe.wait_ge(s["masked"], NSEL * n + SEL_BY[k])
                for kb, col, w in blocks:
                    for j in range(SUBS):
                        last = pe.matmul(acc[c][STRIP * j:STRIP * (j + 1), BANK - w:BANK],
                                         v_grp[par][:, kb, j // 2, :],
                                         e_buf[:, k % ESLOTS, j, col:col + w],
                                         start=k in (0, 3), stop=k in (2, NQ - 1), skip_group_check=True)
                last.then_inc(s["summed"], 1)

            def turn_sums(n, c):
                pe.wait_ge(s["acc_copied"], 2 * n + c + 1)
                for qb in range(4):
                    last = pe.transpose(acc[c][:, P * qb:P * (qb + 1)], o_rows[c][:, P * qb:P * (qb + 1)],
                                        identf[:])
                last.then_inc(s["acc_turned"], 1)

            pe.wait_ge(s["ident"], 5)
            pe.wait_ge(s["x_in"], 16)
            for t in range(NT):
                last = pe.transpose(wide[t // 4][:, P * (t % 4):P * (t % 4 + 1)], x_tok[:, t, :], identf[:])
                if t % 4 == 3:
                    last.then_inc(s["xt_done"], 1)
            pe.wait_ge(s["wqk_in"], 32)
            for ch in range(NCH):
                if ch % 2 == 0:
                    pe.wait_ge(s["xt_copied_a"], ch // 2 + 1)
                else:
                    pe.wait_ge(s["xt_copied_d"], ch // 2 + 1)
                for w, weights in enumerate((wq_sb, wk_sb)):
                    m = 2 * ch + w
                    wait(pe, s["rest_done"], m - 3)
                    pe.matmul(narrow[m % 4], weights[:], xT[:, BANK * ch:BANK * (ch + 1)], start=True,
                              stop=True).then_inc(s["proj_done"], 1)
            pe.wait_ge(s["wv_in"], 16)
            for t in range(NT):
                last = pe.matmul(wide[t // 4][:, P * (t % 4):P * (t % 4 + 1)], xT[:, P * t:P * (t + 1)],
                                 wv_sb[:], start=True, stop=True)
                if t % 4 == 3:
                    last.then_inc(s["v_done"], 1)
            pe.wait_ge(s["w_in"], 16 * 4)
            pe.wait_ge(s["v_copied"], NCH)
            for i in range(3):
                last = pe.transpose(wide[0][:, P * i:P * (i + 1)], wf_sb[:, i, :], identf[:])
            last.then_inc(s["wt_done"], 1)

            pe.wait_ge(s["mask_set"], 1)
            pe.wait_ge(s["rest_done"], 2 * NCH)
            for k in range(NU):
                max_unit(0, 0, k)
            turn_maxima(0, 0)
            for k in range(EARLY):
                max_unit(1, 1, k)
            pe.wait_ge(s["wvt_copied"], 1)
            pe.wait_ge(s["wt_scaled"], 4)

            def group(n, par):
                static = isinstance(n, int)
                for k in range(NQ):
                    if k < TQUAD:
                        units = [] if static and n + 1 >= NG else \
                            [(n + 1, 1 - par, EARLY + sum(UNITS_AT[:k]) + u) for u in range(UNITS_AT[k])]
                    else:
                        units = [] if static and n + 2 >= NG else \
                            [(n + 2, par, sum(UNITS_AT[TQUAD:k]) + u) for u in range(UNITS_AT[k])]
                    turn = k == TQUAD and not (static and n + 1 >= NG)
                    before = 0 if turn else len(units) - 1
                    for u in units[:min(before, 1)]:
                        max_unit(*u)
                    score_pair(n, par, k, 0)
                    for u in units[1:min(before, 2)]:
                        max_unit(*u)
                    score_pair(n, par, k, 1)
                    for u in units[2:before]:
                        max_unit(*u)
                    if k == 0:
                        if not (static and n == 0):
                            sum_quad(n - 1, 1 - par, NQ - 1)
                    else:
                        sum_quad(n, par, k - 1)
                    if k == 1 and not (static and n == 0):
                        turn_sums(n - 1, 1)
                    if k == 4:
                        turn_sums(n, 0)
                    if turn:
                        turn_maxima(n + 1, 1 - par)
                    for u in units[before:]:
                        max_unit(*u)

            group(0, 0)
            group(1, 1)
            with pe.Fori(1, NG // 2 - 1) as i:
                group(2 * i, 0)
                group(2 * i + 1, 1)
            group(NG - 2, 0)
            group(NG - 1, 1)
            sum_quad(NG - 1, 1, NQ - 1)
            turn_sums(NG - 1, 1)

            attn_tiles = attn_n[:].rearrange("p (q b e) -> p b q e", q=NB, b=B)
            pe.wait_ge(s["attn_ready"], NG)
            for ch in range(NCH):
                for i in range(4):
                    t = 4 * ch + i
                    last = pe.transpose(wide[ch][:, P * i:P * (i + 1)], attn_tiles[:, t // NB, t % NB, :],
                                        identf[:])
                last.then_inc(s["a_turned"], 1)
            pe.wait_ge(s["rms_done"], 2)
            for ch in range(NCH):
                pe.wait_ge(s["a_copied"], ch + 1)
                if ch == 0:
                    pe.wait_ge(s["o_stored"], 2 * NG)
                for i in range(4):
                    last = pe.matmul(narrow[ch][:, P * i:P * (i + 1)], attnT[:, ch, P * i:P * (i + 1)],
                                     wo_scaled[:], start=True, stop=True)
                last.then_inc(s["a_projected"], 1)
            for ch in range(NCH):
                pe.wait_ge(s["x1_ready"], ch + 1)
                for i in range(4):
                    last = pe.transpose(wide[ch][:, P * i:P * (i + 1)], x1[:, 4 * ch + i, :], identf[:])
                last.then_inc(s["x1_turned"], 1)
            pe.wait_ge(s["xcol_set"], 1)
            for ch in range(NCH):
                b, t0 = ch * BANK // S, ch * BANK % S
                pe.wait_ge(s["x1_copied"], ch + 1)
                pe.wait_ge(s["y_added"], ch + 1)
                pe.matmul(narrow[ch], w_cur[:, 1, :], x1T[:, b, 1 + t0:1 + t0 + BANK], start=True, stop=False)
                pe.matmul(narrow[ch], w_prev[:, 1, :], x1T[:, b, t0:t0 + BANK], start=False, stop=True)\
                    .then_inc(s["k_scored"], 1)
                for i in range(4):
                    o = wide[ch][:, P * i:P * (i + 1)]
                    t1 = t0 + P * i
                    pe.matmul(o, x1T[:, b, 1 + t1:1 + t1 + P], w_cur[:, 0, :], start=True, stop=False)
                    last = pe.matmul(o, x1T[:, b, t1:t1 + P], w_prev[:, 0, :], start=False, stop=True)
                last.then_inc(s["r_scored"], 1)
            for ch in range(NCH):
                pe.wait_ge(s["k_squared"], ch + 1)
                for i in range(4):
                    last = pe.matmul(narrow[ch][:, P * i:P * (i + 1)], k_act[:, ch, P * i:P * (i + 1)], wvT[:],
                                     start=True, stop=True)
                last.then_inc(s["o_scored"], 1)

        @block.scalar
        def _(act):
            act.dma_start(wo_sb[:], Wo).then_inc(s["w_in"], 16)
            for i, w in enumerate((W_r, W_k, W_v)):
                act.dma_start(wf_sb[:, i, :], w).then_inc(s["w_in"], 16)
            for i, m in enumerate((mu_r, mu_k)):
                act.dma_start(mu[:, i:i + 1], m.unsqueeze(1)).then_inc(s["small_in"], 16)
            for i, l in enumerate((lq1, lq2, lk1, lk2)):
                act.dma_start(lam_in[:, i, :], l.partition_broadcast(P)).then_inc(s["small_in"], 16)
            act.dma_start(w_bounce, rms_w.partition_broadcast(HEADS)).then_inc(s["bounce_in"], 16)
            act.wait_ge(s["bounce_in"], 16)
            act.dma_start(rms_col[:], w_bounce.rearrange("h w -> (h w)").unsqueeze(1)).then_inc(s["small_in"], 16)

            for ch in range(0, NCH, 2):
                act.wait_ge(s["xt_done"], ch + 1)
                nc.scalar.copy(xT[:, BANK * ch:BANK * (ch + 1)], wide[ch]).then_inc(s["xt_copied_a"], 1)

            def high(m):
                act.wait_ge(s["proj_done"], m + 1)
                nc.scalar.activation(parts[m % 2][0][:].rearrange("p b t -> p (b t)")[:, BANK * (m // 2):BANK * (m // 2 + 1)],
                                     narrow[m % 4], ACT.Copy, scale=SCALE if m % 2 == 0 else 1.0)\
                    .then_inc(s["hi_done"], 1)

            def middle(m):
                act.wait_ge(s["rest_done"], m + 1)
                nc.scalar.copy(parts[m % 2][1][:].rearrange("p b t -> p (b t)")[:, BANK * (m // 2):BANK * (m // 2 + 1)],
                               rest[:, m % 4, :]).then_inc(s["mid_done"], 1)

            high(0)
            for m in range(1, 2 * NCH):
                high(m)
                middle(m - 1)
            middle(2 * NCH - 1)
            act.wait_ge(s["lam_dots"], 2)
            nc.scalar.activation(lam_exp[:], lam_sum[:], ACT.Exp).then_inc(s["lam_exped"], 1)
            act.wait_ge(s["wt_done"], 1)
            nc.scalar.copy(wvT[:], wide[0][:, 2 * P:3 * P]).then_inc(s["wvt_copied"], 1)

            def take_sums(n, c):
                act.wait_ge(s["summed"], NQ * n + (3 if c == 0 else NQ))
                wait(act, s["acc_turned"], 2 * n + c - 1)
                nc.scalar.copy(o_rows[c][:], acc[c][:]).then_inc(s["acc_copied"], 1)

            def store_sums(n, par, c):
                act.wait_ge(s["acc_turned"], 2 * n + c + 1)
                wait(act, s["norm_steps"], 9 * (n - 1))
                nc.scalar.copy(o_tok[par][:, 4 * c:4 * c + 4],
                               acc[c][:].rearrange("p (q j w) -> p q j w", q=4, j=SUBS)[:, :, :, 0:VW + 1])\
                    .then_inc(s["o_stored"], 1)

            def group(n, par):
                static = isinstance(n, int)
                for k in range(NQ):
                    used = max(col + w for _, col, w in QUADS[k][1])
                    for p in range(2):
                        act.wait_ge(s["scored"], 2 * NQ * n + 2 * k + p + 1)
                        if p == 0:
                            wait(act, s["summed"], NQ * n + k - ESLOTS + 1)
                        nc.scalar.activation(e_buf[:, k % ESLOTS, 2 * p:2 * p + 2, 0:used], ex[p][:, :, 0:used],
                                             ACT.Exp).then_inc(s["exped"], 1)
                    if k == 0 and not (static and n == 0):
                        take_sums(n - 1, 1)
                    if k == 2 and not (static and n == 0):
                        store_sums(n - 1, 1 - par, 1)
                    if k == 3:
                        take_sums(n, 0)
                    if k == 5:
                        store_sums(n, par, 0)

            group(0, 0)
            group(1, 1)
            with act.Fori(1, NG // 2 - 1) as i:
                group(2 * i, 0)
                group(2 * i + 1, 1)
            group(NG - 2, 0)
            group(NG - 1, 1)
            take_sums(NG - 1, 1)
            store_sums(NG - 1, 1, 1)

            for ch in range(NCH):
                act.wait_ge(s["a_turned"], ch + 1)
                nc.scalar.copy(attnT[:, ch, :], wide[ch]).then_inc(s["a_copied"], 1)
            for ch in range(NCH):
                b, t0 = ch * BANK // S, ch * BANK % S
                act.wait_ge(s["x1_turned"], ch + 1)
                nc.scalar.copy(x1T[:, b, 1 + t0:1 + t0 + BANK], wide[ch]).then_inc(s["x1_copied"], 1)
            for ch in range(NCH):
                act.wait_ge(s["k_scored"], ch + 1)
                nc.scalar.activation(k_relu[:, ch, :], narrow[ch], ACT.Relu).then_inc(s["k_relued"], 1)
                act.wait_ge(s["r_scored"], ch + 1)
                nc.scalar.activation(r_gate[:, ch, :], wide[ch], ACT.Sigmoid).then_inc(s["r_gated"], 1)

        @block.vector
        def _(dve):
            for ch in range(1, NCH, 2):
                dve.wait_ge(s["xt_done"], ch + 1)
                nc.vector.tensor_copy(xT[:, BANK * ch:BANK * (ch + 1)], wide[ch]).then_inc(s["xt_copied_d"], 1)

            def remainder(m):
                dve.wait_ge(s["hi_done"], m + 1)
                wait(dve, s["lo_done"], m - 3)
                hi = parts[m % 2][0][:].rearrange("p b t -> p (b t)")[:, BANK * (m // 2):BANK * (m // 2 + 1)]
                nc.vector.scalar_tensor_tensor(out=rest[:, m % 4, :], in0=narrow[m % 4],
                                               scalar=SCALE if m % 2 == 0 else 1.0, in1=hi, op0=ALU.mult,
                                               op1=ALU.subtract).then_inc(s["rest_done"], 1)

            def low(m):
                dve.wait_ge(s["mid_done"], m + 1)
                cols = slice(BANK * (m // 2), BANK * (m // 2 + 1))
                mid, lo = (parts[m % 2][a][:].rearrange("p b t -> p (b t)")[:, cols] for a in (1, 2))
                nc.vector.tensor_tensor(lo, rest[:, m % 4, :], mid, ALU.subtract).then_inc(s["lo_done"], 1)

            remainder(0)
            for m in range(1, 2 * NCH):
                remainder(m)
                low(m - 1)
            low(2 * NCH - 1)
            for ch in range(NCH):
                b, kb = ch // 2, ch % 2 * 4
                dve.wait_ge(s["v_done"], ch + 1)
                src = wide[ch].rearrange("p (k g w) -> p k g w", k=4, g=GPB)
                dst = v_all[:].rearrange("p (b g k w) -> p b k g w", b=B, g=GPB, k=NB)[:, b, kb:kb + 4]
                nc.vector.tensor_copy(dst, src).then_inc(s["v_copied"], 1)
            dve.wait_ge(s["small_in"], 16 * 7)
            nc.vector.tensor_tensor(lam_prod[:], lam_in[:, 0:2, :], lam_in[:, 2:4, :], ALU.mult)\
                .then_inc(s["lam_dots"], 1)
            dve.wait_ge(s["lam_dots"], 1)
            nc.vector.tensor_reduce(lam_sum[:], lam_prod[:], AX.X, ALU.add).then_inc(s["lam_dots"], 1)
            nc.vector.tensor_scalar(rms_scaled[:], rms_col[:], (1.0 - LAMBDA_INIT) * VW ** 0.5, None, ALU.mult)\
                .then_inc(s["rms_done"], 1)
            nc.vector.tensor_scalar(mu1[:], mu[:], -1.0, 1.0, ALU.mult, ALU.add).then_inc(s["wt_scaled"], 1)
            dve.wait_ge(s["rms_done"], 1)
            dve.wait_ge(s["w_in"], 16 * 4)
            nc.vector.tensor_scalar(wo_scaled[:], wo_sb[:], rms_scaled[:], None, ALU.mult).then_inc(s["rms_done"], 1)
            dve.wait_ge(s["lam_exped"], 1)
            nc.vector.scalar_tensor_tensor(out=lam_neg[:], in0=lam_exp[:, 1:2], scalar=-LAMBDA_INIT,
                                           in1=lam_exp[:, 0:1], op0=ALU.add, op1=ALU.subtract)\
                .then_inc(s["lam_done"], 1)
            dve.wait_ge(s["lam_done"], 1)
            nc.vector.memset(lam_pair[:, 0::2], 1.0).then_inc(s["lam_paired"], 1)
            nc.vector.tensor_copy(lam_pair[:, 1::2], lam_neg[:].broadcast_to([P, NB * SUBS // 2]))\
                .then_inc(s["lam_paired"], 1)
            dve.wait_ge(s["wt_done"], 1)
            dve.wait_ge(s["wvt_copied"], 1)
            dve.wait_ge(s["wt_scaled"], 1)
            for i in range(2):
                src = wide[0][:, P * i:P * (i + 1)]
                nc.vector.tensor_scalar(w_cur[:, i, :], src, mu[:, i:i + 1], None, ALU.mult)
                nc.vector.tensor_scalar(w_prev[:, i, :], src, mu1[:, i:i + 1], None, ALU.mult)\
                    .then_inc(s["wt_scaled"], 1)
            dve.wait_ge(s["wt_scaled"], 3)
            nc.vector.memset(far_max[:], 0.0).then_inc(s["wt_scaled"], 1)

            def max_unit(n, par, k):
                dve.wait_ge(s["max_scored"], NU * n + k + 1)
                u, j = divmod(k, SUBS)
                if k == 0:
                    wait(dve, s["combined"], 5 * n)
                nc.vector.tensor_reduce(part_max[:, j, u, :],
                                        mx[(par + k) % 2][:].rearrange("p (a b) -> p a b", a=4), AX.X, ALU.max)\
                    .then_inc(s["maxed"], 1)

            def copy_maxima(n, par):
                wait(dve, s["max_rows_in"], 32 * n)
                dve.wait_ge(s["negmax_turned"], n + 1)
                nc.vector.tensor_copy(max_rows[:], mx[(par + NU) % 2][0:2 * SUBS, :].bitcast(BF16))\
                    .then_inc(s["negmax_copied"], 1)

            def combine(n):
                dve.wait_ge(s["maxed"], NU * (n + 1))
                wait(dve, s["negmax_done"], n)
                wait(dve, s["negmax_turned"], n)
                nc.vector.tensor_reduce(row_max[:, :, 2:8:4], part_max[:, :, 0:2, 1:4], AX.X, ALU.max)\
                    .then_inc(s["combined"], 1)
                nc.vector.tensor_reduce(row_max[:, :, 3:8:4], part_max[:, :, 2:4, :], AX.X, ALU.max)\
                    .then_inc(s["combined"], 1)
                nc.vector.tensor_reduce(row_max[:, :, 1:8:4],
                                        part_max[:, :, 8, :].rearrange("p j (a b) -> p j a b", a=2),
                                        AX.X, ALU.max).then_inc(s["combined"], 1)
                nc.vector.tensor_copy(row_max[:, :, 0:8:4], part_max[:, :, 0:2, 0]).then_inc(s["combined"], 1)
                nc.vector.tensor_reduce(far_max[:], part_max[:, :, 4:8, :], AX.X, ALU.max)\
                    .then_inc(s["combined"], 1)
                dve.wait_ge(s["combined"], 5 * n + 5)
                nc.vector.tensor_tensor(row_max[:, :, 4:8], row_max[:, :, 4:8], far_max[:], ALU.max)\
                    .then_inc(s["normed_d"], 1)
                dve.wait_ge(s["normed_d"], 2 * n + 1)
                nc.vector.tensor_scalar(neg_max[:, 0], row_max[:], -1.0, None, ALU.mult).then_inc(s["normed_d"], 1)
                dve.wait_ge(s["normed_d"], 2 * n + 2)
                nc.vector.scalar_tensor_tensor(out=neg_max[:, 1], in0=row_max[:], scalar=-1.0,
                                               in1=neg_max[:, 0], op0=ALU.mult, op1=ALU.subtract)\
                    .then_inc(s["negmax_done"], 1)

            for k in range(NU):
                max_unit(0, 0, k)
            combine(0)
            copy_maxima(0, 0)
            for k in range(EARLY):
                max_unit(1, 1, k)

            def invert(n, par):
                dve.wait_ge(s["o_stored"], 2 * n + 2)
                wait(dve, s["norm_steps"], 9 * (n - 1))
                nc.vector.reciprocal(r_den[par][:].rearrange("p (q j) -> p q j", j=SUBS), o_tok[par][:, :, :, VW])\
                    .then_inc(s["den_inverted"], 1)

            def group(n, par):
                static = isinstance(n, int)
                if not (static and n + 1 >= NG):
                    for k in range(EARLY, NU):
                        max_unit(n + 1, 1 - par, k)
                        if k == EARLY + sum(UNITS_AT[:4]) and not (static and n == 0):
                            invert(n - 1, 1 - par)
                    combine(n + 1)
                    copy_maxima(n + 1, 1 - par)
                if not (static and n + 2 >= NG):
                    for k in range(EARLY):
                        max_unit(n + 2, par, k)

            group(0, 0)
            group(1, 1)
            with dve.Fori(1, NG // 2 - 1) as i:
                group(2 * i, 0)
                group(2 * i + 1, 1)
            group(NG - 2, 0)

            invert(NG - 2, 0)
            invert(NG - 1, 1)

            def layer_norm(src, st, mv, ve, rs, dst, ch, stats, rooted, ready):
                for i in range(4):
                    nc.vector.bn_stats(st[:, 4 * ch + i, :], src[:, 4 * ch + i, :]).then_inc(stats, 1)
                dve.wait_ge(stats, 9 * ch + 4)
                for i in range(4):
                    nc.vector.bn_aggr(mv[:, 4 * ch + i, :], st[:, 4 * ch + i, :]).then_inc(stats, 1)
                dve.wait_ge(stats, 9 * ch + 8)
                nc.vector.tensor_scalar(ve[:, 4 * ch:4 * ch + 4], mv[:, 4 * ch:4 * ch + 4, 1], LN_EPS, None,
                                        ALU.add).then_inc(stats, 1)
                dve.wait_ge(rooted, ch + 1)
                for i in range(4):
                    t = 4 * ch + i
                    last = nc.vector.tensor_scalar(dst[:, t, :], src[:, t, :], mv[:, t, 0:1], rs[:, t:t + 1],
                                                   ALU.subtract, ALU.mult)
                last.then_inc(ready, 1)

            for ch in range(NCH):
                dve.wait_ge(s["a_projected"], ch + 1)
                nc.vector.tensor_tensor(y[:, 4 * ch:4 * ch + 4, :], narrow[ch].rearrange("p (t c) -> p t c", t=4),
                                        x_tok[:, 4 * ch:4 * ch + 4, :], ALU.add).then_inc(s["y_added"], 1)
                dve.wait_ge(s["y_added"], ch + 1)
                layer_norm(y, st1, mv1, ve1, rs1, x1, ch, s["stats1"], s["rooted1"], s["x1_ready"])
            for ch in range(NCH):
                dve.wait_ge(s["k_relued"], ch + 1)
                nc.vector.tensor_tensor(k_act[:, ch, :], k_relu[:, ch, :], k_relu[:, ch, :], ALU.mult)\
                    .then_inc(s["k_squared"], 1)
            for ch in range(NCH):
                dve.wait_ge(s["r_gated"], ch + 1)
                dve.wait_ge(s["o_scored"], ch + 1)
                nc.vector.tensor_tensor(z0[:, ch, :], narrow[ch], r_gate[:, ch, :], ALU.mult)\
                    .then_inc(s["z_steps"], 1)
                dve.wait_ge(s["z_steps"], ch + 1)
                nc.vector.tensor_tensor(z[:, 4 * ch:4 * ch + 4, :], z0[:, ch, :].rearrange("p (t c) -> p t c", t=4),
                                        x1[:, 4 * ch:4 * ch + 4, :], ALU.add).then_inc(s["z_ready"], 1)
                dve.wait_ge(s["z_ready"], ch + 1)
                layer_norm(z, st2, mv2, ve2, rs2, res, ch, s["stats2"], s["rooted2"], s["out_ready"])


_INS = ["L0_attn_x", "L0_attn_Wq", "L0_attn_Wk", "L0_attn_Wv", "L0_attn_Wo", "L0_attn_lq1", "L0_attn_lk1",
        "L0_attn_lq2", "L0_attn_lk2", "L0_attn_rms_w", "L0_ffn_W_r", "L0_ffn_W_k", "L0_ffn_W_v",
        "L0_ffn_mu_r", "L0_ffn_mu_k"]


def kernel(**inputs):
    import numpy as _np
    import concourse.bacc as _bacc
    from concourse import mybir as _mybir
    from concourse.bass_utils import run_bass_kernel_spmd as _run

    nc = _bacc.Bacc("TRN2", target_bir_lowering=False, num_devices=1)
    arrays, args = {}, []
    for name in _INS:
        a = _np.ascontiguousarray(inputs[name])
        arrays[f"in_{name}"] = a
        args.append(nc.dram_tensor(f"in_{name}", a.shape, _mybir.dt.from_np(a.dtype), kind="ExternalInput").ap())
    shape = inputs["L0_attn_x"].shape
    args.append(nc.dram_tensor("out_0", shape, _mybir.dt.float32, kind="ExternalOutput").ap())
    build(nc, *args)
    r = _run(nc, [arrays], core_ids=[0])
    return r.results[0]["out_0"]
```

```python
import math
from contextlib import ExitStack

import concourse.bass as bass
from concourse import mybir

F32 = mybir.dt.float32
BF16 = mybir.dt.bfloat16
ALU = mybir.AluOpType
ACT = mybir.ActivationFunctionType
AX = mybir.AxisListType

P = 128
BANK = 512
HEADS = 16
D = P // HEADS // 2
VW = 2 * D
SUBS = 4
STRIP = 32
VPAD = STRIP // 2
LAMBDA_INIT = 0.8 - 0.6 * math.exp(-0.3 * 12)
RMS_EPS = 1e-5
LN_EPS = 1e-5
NEG = -1e30

TERMS = [(0, 1), (0, 2), (0, 0), (1, 0), (2, 0), (1, 1)]
ROW_GROUP = STRIP // D
FILL = len(TERMS)

MAX_UNITS = [
    ([(0, 2, 0, 3), (384, 0, 0, 1)], [(256, 2)]),
    ([(0, 6, 4, 3), (384, 4, 4, 1)], [(256, 2)]),
    ([(0, 3, 0, 4)], [(384, 1)]),
    ([(0, 7, 4, 4)], [(384, 1)]),
    ([(0, 4, 0, 4)], []),
    ([(0, 5, 0, 4)], []),
    ([(0, 6, 0, 4)], []),
    ([(0, 7, 0, 4)], []),
    ([(0, 1, 0, 2), (256, 5, 4, 2)], [(128, 1), (384, 1)]),
]
NU = len(MAX_UNITS) * SUBS

QUADS = [
    (0, [(0, 0, 512)]),
    (0, [(1, 0, 384), (3, 384, 128)]),
    (0, [(2, 0, 256)]),
    (1, [(0, 0, 512)]),
    (1, [(1, 0, 512)]),
    (1, [(2, 0, 512)]),
    (1, [(3, 0, 512)]),
    (1, [(4, 0, 512)]),
    (1, [(5, 0, 384), (7, 384, 128)]),
    (1, [(6, 0, 256)]),
]
NQ = len(QUADS)
ESLOTS = 5
DIAG = [[col for kb, col, w in parts if kb // 4 == c] for c, parts in QUADS]
NSEL = sum(map(len, DIAG))
SEL_BY = [sum(map(len, DIAG[: k + 1])) for k in range(NQ)]

EARLY = 8
TQUAD = 7
TURNED = 2
LAG = 2
UNITS_AT = [4, 4, 4, 4, 4, 4, 4, 2, 4, 2]
assert sum(UNITS_AT[:TQUAD]) == NU - EARLY and sum(UNITS_AT[TQUAD:]) == EARLY


def wait(eng, sem, value):
    if isinstance(value, int) and value <= 0:
        return
    eng.wait_ge(sem, value)


def build(nc, x, Wq, Wk, Wv, Wo, lq1, lk1, lq2, lk2, rms_w, W_r, W_k, W_v, mu_r, mu_k, out):
    B, S, _ = x.shape
    NB = S // P
    NT = B * NB
    NCH = NT * P // BANK
    GPB = 2 * HEADS // SUBS
    NG = B * GPB
    NSUB = NG * SUBS
    SCALE = D ** -0.5

    q_rows = nc.dram_tensor("q_rows", (NSUB, STRIP, S), BF16, kind="Internal").ap()
    k_rows = nc.dram_tensor("k_rows", (NSUB, STRIP, S), BF16, kind="Internal").ap()
    w_bounce = nc.dram_tensor("w_bounce", (HEADS, VW), F32, kind="Internal").ap()
    q_group = q_rows.rearrange("(n j) r t -> n (j r) t", j=SUBS)
    k_group = k_rows.rearrange("(n j) r t -> n (j r) t", j=SUBS)
    q_parts = q_rows.rearrange("s (d g) t -> (s d) g t", g=ROW_GROUP)
    k_parts = k_rows.rearrange("s (d g) t -> (s d) g t", g=ROW_GROUP)
    q_subs = q_rows.rearrange("(n j) r t -> n j r t", j=SUBS)
    HEAD = 2 * SUBS * D
    MAX_LOADS = 16 * (SUBS + 1)
    EXP_LOADS = 16 * 2
    x_tiles = x.rearrange("b (n p) c -> p (b n) c", p=P)
    out_tiles = out.rearrange("b (n p) c -> p (b n) c", p=P)

    with ExitStack() as ctx:
        def sb(name, shape, dt=F32):
            return ctx.enter_context(nc.sbuf_tensor(name, shape, dt))

        def sem(name):
            return ctx.enter_context(nc.semaphore(name))

        x_tok = sb("x_tok", [P, NT, P])
        xT = sb("xT", [P, NT * P])
        wq_sb, wk_sb, wv_sb, wo_sb = (sb(n, [P, P]) for n in ("wq_sb", "wk_sb", "wv_sb", "wo_sb"))
        wf_sb = sb("wf_sb", [P, 3, P])
        wo_scaled = sb("wo_scaled", [P, P])
        w_cur = sb("w_cur", [P, 2, P])
        w_prev = sb("w_prev", [P, 2, P])
        wvT = sb("wvT", [P, P])
        mu = sb("mu", [P, 2])
        mu1 = sb("mu1", [P, 2])
        rms_col = sb("rms_col", [P, 1])
        rms_scaled = sb("rms_scaled", [P, 1])
        lam_in = sb("lam_in", [P, 4, D])
        lam_prod = sb("lam_prod", [P, 2, D])
        lam_sum = sb("lam_sum", [P, 2])
        lam_exp = sb("lam_exp", [P, 2])
        lam_neg = sb("lam_neg", [P, 1])
        identf = sb("identf", [P, P])
        identb = sb("identb", [P, P], BF16)
        ones_rows = sb("ones_rows", [P, S], BF16)
        zero_rows = sb("zero_rows", [P, S], BF16)
        mask_zero = sb("mask_zero", [P, 2, P], BF16)
        mask = sb("mask", [P, 2, P], BF16)
        parts = [[sb(f"part_{w}{a}", [P, B, S], BF16) for a in range(3)] for w in "qk"]
        rest = sb("rest", [P, 4, BANK])
        v_all = sb("v_all", [P, NG * NB * 2 * VW])
        v_grp = [sb(f"v_grp{i}", [P, NB, 2, STRIP + VPAD]) for i in range(2)]
        qm = [sb(f"qm{i}", [P, SUBS, S], BF16) for i in range(2)]
        km = [sb(f"km{i}", [P, S], BF16) for i in range(2)]
        qe = [sb(f"qe{i}", [P, S], BF16) for i in range(2)]
        ke = [sb(f"ke{i}", [P, S], BF16) for i in range(2)]
        part_max = sb("part_max", [P, SUBS, 2, 4])
        far_max = sb("far_max", [P, SUBS, 4])
        row_max = sb("row_max", [P, SUBS, NB])
        neg_max = sb("neg_max", [P, 2, SUBS, NB], BF16)
        max_rows = sb("max_rows", [2 * SUBS, S], BF16)
        e_buf = sb("e_buf", [P, ESLOTS, SUBS, BANK])
        o_rows = [sb(f"o_rows{i}", [P, BANK]) for i in range(2)]
        o_tok = [sb(f"o_tok{i}", [P, NB * SUBS, VW + 1]) for i in range(2)]
        r_den = [sb(f"r_den{i}", [P, NB * SUBS]) for i in range(2)]
        lam_pair = sb("lam_pair", [P, NB * SUBS])
        r_lam = sb("r_lam", [P, NB * SUBS])
        o_scaled = sb("o_scaled", [P, NB * SUBS, VW])
        attn = sb("attn", [P, NB * 2, VW])
        attn_sq = sb("attn_sq", [P, NB * 2, VW])
        sq4 = sb("sq4", [P, NB * 2, 4])
        sq2 = sb("sq2", [P, NB * 2, 2])
        sq1 = sb("sq1", [P, NB * 2])
        sq_eps = sb("sq_eps", [P, NB * 2])
        r_rms = sb("r_rms", [P, NB * 2])
        eps_tile = sb("eps_tile", [P, NB * 2])
        attn_n = sb("attn_n", [P, NB * NG * 2 * VW])

        ex = [ctx.enter_context(nc.psum_tensor(f"ex{i}", [P, 2, BANK], F32)) for i in range(2)]
        acc = [ctx.enter_context(nc.psum_tensor(f"acc{i}", [P, BANK], F32)) for i in range(2)]
        mx = [ctx.enter_context(nc.psum_tensor(f"mx{i}", [P, BANK], F32)) for i in range(2)]
        wide = [ex[0][:, 0, :], ex[0][:, 1, :], ex[1][:, 0, :], ex[1][:, 1, :]]
        narrow = [acc[0][:], acc[1][:], mx[0][:], mx[1][:]]

        main = [narrow[2], narrow[3], narrow[2], wide[0]]
        side = [main[0], main[1], wide[2], wide[3]]

        pairs = o_scaled[:].rearrange("p (a s c) w -> p a s (c w)", s=2, c=2)
        attn_chunks = attn[:].rearrange("p (b h c) w -> p c b h w", b=NB // 2, h=2)
        r_rms_chunks = r_rms[:].rearrange("p (b h c) -> p c b h", b=NB // 2, h=2).unsqueeze(4)\
            .broadcast_to([P, 2, NB // 2, 2, VW])
        attn_out = attn_n[:].rearrange("p (c b n h w) -> p n c b h w", c=2, b=NB // 2, n=NG, h=2)

        names = """x_in0 x_in1 wqk_in wv_in w_in small_in bounce_in rms_in
                   ident ones_set mask_set vpad_set xcol_set
                   xt_done xt_copied_a xt_copied_d proj_done hi_done rest_done mid_done lo_done
                   v_done v_copied wt_done mu_ready wt_scaled lam_dots lam_exped lam_done rms_done
                   rows_head rows_b0 rows_b1 qkm_in0 qkm_in1 qke_in0 qke_in1 max_rows_in v_grp_set
                   max_scored maxed combined negmax_done negmax_turned negmax_copied
                   scored exped masked summed acc_copied acc_turned o_stored
                   normed_d attn_ready a_turned a_copied a_projected y_added stats1 x1_ready
                   x1_turned x1_copied k_scored r_scored k_relued r_gated k_squared o_scored z_scaled z_ready
                   stats2 rooted1 rooted2 half_set half_steps half_rooted shifted1 shifted2 quad_seen
                   stacks_zeroed den_inverted values_seen norm_seen norm_steps lam_paired out_ready
                   out_stored""".split()
        s = {n: sem(n) for n in names}
        s_qkm = [s["qkm_in0"], s["qkm_in1"]]
        s_qke = [s["qke_in0"], s["qke_in1"]]

        def pair_of_chunks(t):
            return t[:].rearrange("p b t -> p (b t)").bitcast(F32).rearrange("p (c t) -> p c t", c=2)

        attnT, k_relu, k_act = map(pair_of_chunks, parts[0])
        r_tanh, z0 = map(pair_of_chunks, parts[1][0:2])
        y = xT[:].rearrange("p (t c) -> p t c", t=NT)
        z = y
        res = v_all[:].rearrange("p (t c) -> p t c", t=NT)
        st1 = sb("st1", [P, NT, 6])
        mv1 = sb("mv1", [P, NT, 2])
        ve1 = sb("ve1", [P, NT])
        rs1 = sb("rs1", [P, NT])
        nm1 = sb("nm1", [P, NT])
        shift1 = sb("shift1", [P, NT])
        x1 = sb("x1", [P, NT, P])
        x1T = sb("x1T", [P, B, 1 + S])
        st2 = sb("st2", [P, NT, 6])
        mv2 = sb("mv2", [P, NT, 2])
        ve2 = sb("ve2", [P, NT])
        rs2 = sb("rs2", [P, NT])
        nm2 = sb("nm2", [P, NT])
        shift2 = sb("shift2", [P, NT])
        minus_half = sb("minus_half", [P, NB * 2])

        block = ctx.enter_context(nc.Block())

        def load_max_rows(sp, n, par):
            wait(sp, s["max_scored"], NU * (n - 1))
            for j in range(SUBS):
                sp.dma_start(qm[par][STRIP * j:STRIP * (j + 1), j, :], q_subs[n][j]).then_inc(s_qkm[par], 16)
            sp.dma_start(km[par][:], k_group[n]).then_inc(s_qkm[par], 16)

        def load_exp_rows(sp, n, par):
            wait(sp, s["scored"], 2 * NQ * (n - 1))
            sp.dma_start(qe[par][:], q_group[n]).then_inc(s_qke[par], 16)
            sp.dma_start(ke[par][:], k_group[n]).then_inc(s_qke[par], 16)

        def place_maxima(sp, n, par, visit):
            wait(sp, s_qke[par], EXP_LOADS * (visit + 1))
            wait(sp, s["negmax_copied"], n + 1)
            for e in range(2):
                sp.dma_start(qe[par][FILL + e:P:STRIP, :], max_rows[SUBS * e:SUBS * (e + 1), :])\
                    .then_inc(s["max_rows_in"], 16)

        @block.sync
        def _(sp):
            sp.dma_start(x_tok[:, 0:NB, :], x_tiles[:, 0:NB, :]).then_inc(s["x_in0"], 16)
            sp.dma_start(x_tok[:, NB:NT, :], x_tiles[:, NB:NT, :]).then_inc(s["x_in1"], 16)
            sp.dma_start(wo_sb[:], Wo).then_inc(s["w_in"], 16)
            for i, w in enumerate((W_r, W_k, W_v)):
                sp.dma_start(wf_sb[:, i, :], w).then_inc(s["w_in"], 16)
            def fill_rows(rows, done):
                for target, fill in ((q_parts, zero_rows), (k_parts, ones_rows)):
                    sp.dma_start(target[rows, FILL:ROW_GROUP, :],
                                 fill[:].unsqueeze(1).broadcast_to([P, ROW_GROUP - FILL, S])).then_inc(done, 16)

            def write_parts(b, own, done):
                rows = slice(b * P + own.start, b * P + own.stop)
                for part, need in ((0, "hi_done"), (1, "mid_done"), (2, "lo_done")):
                    sp.wait_ge(s[need], 4 * (b + 1))
                    for w, target in enumerate((q_parts, k_parts)):
                        at = [i for i, term in enumerate(TERMS) if term[w] == part]
                        step = at[1] - at[0] if len(at) > 1 else 1
                        sp.dma_start(target[rows, at[0]:at[-1] + 1:step, :],
                                     parts[w][part][own, b, :].unsqueeze(1)
                                     .broadcast_to([own.stop - own.start, len(at), S])).then_inc(done, 16)

            sp.wait_ge(s["ones_set"], 2)
            fill_rows(slice(0, P), s["rows_head"])
            for i, m in enumerate((mu_r, mu_k)):
                sp.dma_start(mu[:, i:i + 1], m.unsqueeze(1)).then_inc(s["small_in"], 16)
            for i, l in enumerate((lq1, lq2, lk1, lk2)):
                sp.dma_start(lam_in[:, i, :], l.partition_broadcast(P)).then_inc(s["small_in"], 16)
            sp.dma_start(w_bounce, rms_w.partition_broadcast(HEADS)).then_inc(s["bounce_in"], 16)
            write_parts(0, slice(0, HEAD), s["rows_head"])
            sp.wait_ge(s["rows_head"], 16 * (2 + 6))
            sp.wait_ge(s["stacks_zeroed"], 2)
            load_max_rows(sp, 0, 0)
            write_parts(0, slice(HEAD, P), s["rows_b0"])
            load_max_rows(sp, 1, 1)
            load_exp_rows(sp, 0, 0)
            fill_rows(slice(P, 2 * P), s["rows_b1"])
            write_parts(1, slice(0, P), s["rows_b1"])
            sp.wait_ge(s["bounce_in"], 16)
            sp.dma_start(rms_col[:], w_bounce.rearrange("h w -> (h w)").unsqueeze(1)).then_inc(s["rms_in"], 16)
            place_maxima(sp, 0, 0, 0)

            def group(n, par, visit):
                if not isinstance(n, int) or n + 2 < NG:
                    load_max_rows(sp, n + 2, par)
                if not isinstance(n, int) or n + 1 < NG:
                    load_exp_rows(sp, n + 1, 1 - par)
                    place_maxima(sp, n + 1, 1 - par, visit + par)

            sp.wait_ge(s["rows_b0"], 16 * 6)
            group(0, 0, 0)
            group(1, 1, 0)
            sp.wait_ge(s["rows_b1"], 16 * (2 + 6))
            with sp.Fori(1, NG // 2 - 1) as i:
                group(2 * i, 0, i)
                group(2 * i + 1, 1, i)
            group(NG - 2, 0, NG // 2 - 1)
            group(NG - 1, 1, NG // 2 - 1)
            for c in range(NCH):
                sp.wait_ge(s["out_ready"], c + 1)
                sp.dma_start(out_tiles[:, 4 * c:4 * c + 4, :], res[:, 4 * c:4 * c + 4, :])\
                    .then_inc(s["out_stored"], 16)
            sp.wait_ge(s["out_stored"], 16 * NCH)

        v_view = v_all[:].rearrange("p (n k h w) -> p n k h w", n=NG, k=NB, h=2)

        @block.gpsimd
        def _(pool):
            pool.memset(identf[:], 0.0).then_inc(s["ident"], 1)
            pool.memset(identb[:], 0.0).then_inc(s["ident"], 1)
            pool.memset(mask_zero[:], 0.0).then_inc(s["ident"], 1)
            pool.memset(ones_rows[:], 1.0).then_inc(s["ones_set"], 1)
            pool.memset(zero_rows[:], 0.0).then_inc(s["ones_set"], 1)
            pool.wait_ge(s["ident"], 3)
            for m in (identf, identb):
                pool.affine_select(out=m[:], in_=m[:], compare_op=ALU.not_equal, fill=1.0, base=0,
                                   pattern=[[-1, P]], channel_multiplier=1).then_inc(s["ident"], 1)
            pool.affine_select(out=mask[:], in_=mask_zero[:], compare_op=ALU.is_ge, fill=NEG, base=0,
                               pattern=[[0, 2], [-1, P]], channel_multiplier=1).then_inc(s["mask_set"], 1)
            for stack in qm:
                pool.memset(stack[:].bitcast(mybir.dt.uint32), 0).then_inc(s["stacks_zeroed"], 1)
            for i in range(2):
                pool.memset(v_grp[i][:], 0.0).then_inc(s["vpad_set"], 1)
            pool.wait_ge(s["vpad_set"], 2)
            for i in range(2):
                pool.memset(v_grp[i][:, :, :, VPAD + VW:VPAD + VW + 1], 1.0).then_inc(s["vpad_set"], 1)
            pool.memset(x1T[:, :, 0:1], 0.0).then_inc(s["xcol_set"], 1)
            pool.memset(minus_half[:], -0.5).then_inc(s["half_set"], 1)
            pool.memset(eps_tile[:], VW * RMS_EPS).then_inc(s["half_set"], 1)
            pool.wait_ge(s["half_set"], 2)
            pool.wait_ge(s["vpad_set"], 4)

            def stage_values(n, par):
                if not isinstance(n, int) or n > 1:
                    pool.wait_ge(s["summed"], NQ * (n - 1)).then_inc(s["values_seen"], 1)
                pool.tensor_copy(v_grp[par][:, :, :, VPAD:VPAD + VW], v_view[:, n]).then_inc(s["v_grp_set"], 1)

            pool.wait_ge(s["v_copied"], NCH)
            stage_values(0, 0)
            pool.wait_ge(s["lam_paired"], 2)

            def normalise(n, par):
                steps = 9

                def seen(i):
                    wait(pool, s["norm_steps"], steps * n + i)

                pool.wait_ge(s["den_inverted"], n + 1).then_inc(s["norm_seen"], 1)
                pool.tensor_tensor(r_lam[:], r_den[par][:], lam_pair[:], ALU.mult).then_inc(s["norm_steps"], 1)
                seen(1)
                pool.tensor_tensor(o_scaled[:], o_tok[par][:, :, 0:VW],
                                   r_lam[:].unsqueeze(2).broadcast_to([P, NB * SUBS, VW]),
                                   ALU.mult).then_inc(s["norm_steps"], 1)
                seen(2)
                pool.tensor_tensor(attn[:].rearrange("p (a c) w -> p a (c w)", c=2), pairs[:, :, 0],
                                   pairs[:, :, 1], ALU.add)\
                    .then_inc(s["norm_steps"], 1)
                seen(3)
                pool.tensor_tensor(attn_sq[:], attn[:], attn[:], ALU.mult).then_inc(s["norm_steps"], 1)
                seen(4)
                pool.tensor_tensor(sq4[:], attn_sq[:, :, 0:4], attn_sq[:, :, 4:8], ALU.add)\
                    .then_inc(s["norm_steps"], 1)
                seen(5)
                pool.tensor_tensor(sq2[:], sq4[:, :, 0:2], sq4[:, :, 2:4], ALU.add).then_inc(s["norm_steps"], 1)
                seen(6)
                pool.tensor_tensor(sq1[:], sq2[:, :, 0], sq2[:, :, 1], ALU.add).then_inc(s["norm_steps"], 1)
                seen(7)
                pool.tensor_tensor(sq_eps[:], sq1[:], eps_tile[:], ALU.add).then_inc(s["norm_steps"], 1)
                seen(8)
                pool.tensor_tensor(r_rms[:], sq_eps[:], minus_half[:], ALU.pow).then_inc(s["norm_steps"], 1)
                pool.wait_ge(s["norm_steps"], steps * n + 9).then_inc(s["norm_seen"], 1)
                for c in range(2):
                    pool.tensor_tensor(attn_out[:, n, c], attn_chunks[:, c], r_rms_chunks[:, c], ALU.mult)\
                        .then_inc(s["attn_ready"], 1)

            def group(n, par):
                for k in range(NQ):
                    if DIAG[k]:
                        pool.wait_ge(s["exped"], 2 * NQ * n + 2 * k + 2).then_inc(s["quad_seen"], 1)
                    for col in DIAG[k]:
                        e = e_buf[:, k % ESLOTS, :, col:col + P]
                        pool.affine_select(out=e, in_=e, compare_op=ALU.is_ge, fill=0.0, base=0,
                                           pattern=[[0, SUBS], [1, P]], channel_multiplier=-1)\
                            .then_inc(s["masked"], 1)
                    if k == 2 and not (isinstance(n, int) and n + 1 >= NG):
                        stage_values(n + 1, 1 - par)
                    if isinstance(n, int) and n == NG - 1:
                        for stage, arg in beside.get(k, []):
                            stage(arg)
                    if k == 2 and not (isinstance(n, int) and n == 0):
                        normalise(n - 1, 1 - par)

            def root_half(c):
                pool.wait_ge(s["half_steps"], 7 * c + 7)
                pool.tensor_tensor(r_rms[:, c::2], sq_eps[:, c::2], minus_half[:, c::2], ALU.pow)\
                    .then_inc(s["half_rooted"], 1)

            def root(ch, ve, rs, stats, rooted):
                pool.wait_ge(stats, 9 * ch + 9)
                tiles = slice(4 * ch, 4 * ch + 4)
                pool.tensor_tensor(rs[:, tiles], ve[:, tiles], minus_half[:, tiles], ALU.pow).then_inc(rooted, 1)

            def root_and_shift(ch, ve, rs, neg_mean, shift, stats, rooted, shifted):
                root(ch, ve, rs, stats, rooted)
                pool.wait_ge(rooted, ch + 1)
                tiles = slice(4 * ch, 4 * ch + 4)
                pool.tensor_tensor(shift[:, tiles], rs[:, tiles], neg_mean[:, tiles], ALU.mult).then_inc(shifted, 1)

            def root1(ch):
                if ch < NCH // B:
                    root(ch, ve1, rs1, s["stats1"], s["rooted1"])
                else:
                    root_and_shift(ch, ve1, rs1, nm1, shift1, s["stats1"], s["rooted1"], s["shifted1"])

            def root2(ch):
                if ch < NCH // B:
                    root(ch, ve2, rs2, s["stats2"], s["rooted2"])
                else:
                    root_and_shift(ch, ve2, rs2, nm2, shift2, s["stats2"], s["rooted2"], s["shifted2"])

            beside = {0: [(root1, 0)], 2: [(root1, 1)], 6: [(root2, 0)], 7: [(root_half, 0)]}

            group(0, 0)
            group(1, 1)
            with pool.Fori(1, NG // 2 - 1) as i:
                group(2 * i, 0)
                group(2 * i + 1, 1)
            group(NG - 2, 0)
            group(NG - 1, 1)
            for stage, arg in ((root2, 1), (root_half, 1), (root1, 2), (root1, 3), (root2, 2), (root2, 3)):
                stage(arg)

        @block.tensor
        def _(pe):
            def loaded(n, par, loads):
                return loads * (n // 2 + 1) if isinstance(n, int) else loads // 2 * (n - par) + loads

            def max_unit(n, par, k):
                matmuls, diags = MAX_UNITS[k // SUBS]
                j = k % SUBS
                bank = mx[k % 2]
                if k == 0:
                    wait(pe, s_qkm[par], loaded(n, par, MAX_LOADS))
                wait(pe, s["maxed"], NU * n + k - 1)
                for i, (col, nd) in enumerate(diags):
                    pe.matmul(bank[:, col:col + P * nd], identb[:], mask[:, 0:nd, :], start=i == 0, stop=False,
                              skip_group_check=True)
                for i, (col, qb, kb, nk) in enumerate(matmuls):
                    last = pe.matmul(bank[:, col:col + P * nk], qm[par][:, j, P * qb:P * (qb + 1)],
                                     km[par][:, P * kb:P * (kb + nk)], start=not diags and i == 0,
                                     stop=i == len(matmuls) - 1, skip_group_check=True)
                last.then_inc(s["max_scored"], 1)

            def turn_maxima(n, par):
                wait(pe, s["o_stored"], n - 1)
                pe.wait_ge(s["negmax_done"], n + 1)
                turned = acc[par][:].bitcast(BF16)
                for qb in range(NB):
                    last = pe.transpose(turned[0:2 * SUBS, P * qb:P * (qb + 1)],
                                        neg_max[:].rearrange("p e j q -> p q (e j)")[:, qb, :], identb[:])
                last.then_inc(s["negmax_turned"], 1)

            def score_pair(n, par, k, p):
                if k == 0 and p == 0:
                    wait(pe, s_qke[par], loaded(n, par, EXP_LOADS))
                    pe.wait_ge(s["max_rows_in"], 32 * n + 32)
                wait(pe, s["exped"], 2 * NQ * n + 2 * (k - 1) + p + 1)
                c, blocks = QUADS[k]
                q1 = BANK * (c + 1)
                for kb, col, w in blocks:
                    for jj in range(2):
                        rows = slice(STRIP * (2 * p + jj), STRIP * (2 * p + jj + 1))
                        last = pe.matmul(ex[p][:, jj, col:col + w], ke[par][rows, P * kb:P * (kb + 1)],
                                         qe[par][rows, q1 - w:q1], start=True, stop=True)
                last.then_inc(s["scored"], 1)

            def sum_part(n, par, k, half, whole):
                c, blocks = QUADS[k]
                alone = isinstance(n, int) and n == NG - 1 and c == 1
                bank = acc[0] if alone else acc[par]
                shift = 0 if c == 1 else VPAD
                if half == 0:
                    if k == 0:
                        pe.wait_ge(s["v_grp_set"], n + 1)
                        pe.wait_ge(s["negmax_copied"], n + 1)
                    if alone and k == 3:
                        pe.wait_ge(s["o_stored"], NG - 1)
                    pe.wait_ge(s["exped"], 2 * NQ * n + 2 * k + 2)
                    if DIAG[k]:
                        pe.wait_ge(s["masked"], NSEL * n + SEL_BY[k])
                if whole:
                    pieces = [block + (0,) for block in blocks] if half == 0 else []
                elif len(blocks) == 2:
                    pieces = [blocks[half] + (0,)]
                else:
                    kb, col, w = blocks[0]
                    pieces = [(kb, col + half * w // 2, w // 2, 0 if half else w // 2)]
                for kb, col, w, after in pieces:
                    hi = BANK - after
                    for j in range(SUBS):
                        last = pe.matmul(bank[STRIP * j:STRIP * (j + 1), hi - w:hi],
                                         v_grp[par][:, kb, j // 2, shift:shift + STRIP],
                                         e_buf[:, k % ESLOTS, j, col:col + w],
                                         start=half == 0 and k == (3 if alone else 0), stop=k == NQ - 1,
                                         skip_group_check=True)
                if pieces and half == (0 if whole else 1):
                    last.then_inc(s["summed"], 1)

            def turn_sums(n, par):
                pe.wait_ge(s["acc_copied"], n + 1)
                for qb in range(4):
                    last = pe.transpose(acc[par][:, P * qb:P * (qb + 1)], o_rows[par][:, P * qb:P * (qb + 1)],
                                        identf[:])
                last.then_inc(s["acc_turned"], 1)

            pe.wait_ge(s["ident"], 5)
            for b in range(B):
                pe.wait_ge(s[f"x_in{b}"], 16)
                for t in range(b * NB, (b + 1) * NB):
                    last = pe.transpose(wide[t // 4][:, P * (t % 4):P * (t % 4 + 1)], x_tok[:, t, :], identf[:])
                    if t % 4 == 3:
                        last.then_inc(s["xt_done"], 1)
                if b == 0:
                    pe.wait_ge(s["wqk_in"], 32)
                for ch in (2 * b, 2 * b + 1):
                    pe.wait_ge(s["xt_copied_a" if ch % 2 == 0 else "xt_copied_d"], b + 1)
                    for w, weights in enumerate((wq_sb, wk_sb)):
                        m = 2 * ch + w
                        wait(pe, s["rest_done"], m - 3)
                        pe.matmul(narrow[m % 4], weights[:], xT[:, BANK * ch:BANK * (ch + 1)], start=True,
                                  stop=True).then_inc(s["proj_done"], 1)
            pe.wait_ge(s["wv_in"], 16)
            for t in range(NT):
                last = pe.matmul(wide[t // 4][:, P * (t % 4):P * (t % 4 + 1)], xT[:, P * t:P * (t + 1)],
                                 wv_sb[:], start=True, stop=True)
                if t % 4 == 3:
                    last.then_inc(s["v_done"], 1)
            pe.wait_ge(s["w_in"], 16 * 4)
            pe.wait_ge(s["v_copied"], NCH)
            for i in range(3):
                last = pe.transpose(wide[0][:, P * i:P * (i + 1)], wf_sb[:, i, :], identf[:])
            last.then_inc(s["wt_done"], 1)

            pe.wait_ge(s["mask_set"], 1)
            pe.wait_ge(s["rest_done"], 2 * NCH)
            for k in range(NU):
                max_unit(0, 0, k)
            max_unit(1, 1, 0)
            max_unit(1, 1, 1)
            turn_maxima(0, 0)
            for k in range(2, EARLY):
                max_unit(1, 1, k)
            pe.wait_ge(s["wt_scaled"], 1)

            attn_tiles = attn_n[:].rearrange("p (q b e) -> p b q e", q=NB, b=B)

            def turn_attn(ch):
                pe.wait_ge(s["attn_ready"], (2 * GPB, 2 * GPB, 2 * NG - 1, 2 * NG)[ch])
                if ch == 0:
                    pe.wait_ge(s["maxed"], NU * NG)
                if ch == 2:
                    pe.wait_ge(s["z_scaled"], 1)
                for i in range(4):
                    t = 4 * ch + i
                    last = pe.transpose(main[ch][:, P * i:P * (i + 1)], attn_tiles[:, t // NB, t % NB, :],
                                        identf[:])
                last.then_inc(s["a_turned"], 1)

            def project(ch):
                pe.wait_ge(s["rms_done"], 2)
                pe.wait_ge(s["a_copied"], ch + 1)
                for i in range(4):
                    last = pe.matmul(main[ch][:, P * i:P * (i + 1)], attnT[:, ch % 2, P * i:P * (i + 1)],
                                     wo_scaled[:], start=True, stop=True)
                last.then_inc(s["a_projected"], 1)

            def turn_x1(ch):
                pe.wait_ge(s["x1_ready"], ch + 1)
                for i in range(4):
                    last = pe.transpose(main[ch][:, P * i:P * (i + 1)], x1[:, 4 * ch + i, :], identf[:])
                last.then_inc(s["x1_turned"], 1)

            def ffn_k(ch):
                b, t0 = ch * BANK // S, ch * BANK % S
                pe.wait_ge(s["xcol_set"], 1)
                pe.wait_ge(s["x1_copied"], ch + 1)
                pe.matmul(main[ch], w_cur[:, 1, :], x1T[:, b, 1 + t0:1 + t0 + BANK], start=True, stop=False)
                pe.matmul(main[ch], w_prev[:, 1, :], x1T[:, b, t0:t0 + BANK], start=False, stop=True)\
                    .then_inc(s["k_scored"], 1)

            def ffn_r(ch):
                b, t0 = ch * BANK // S, ch * BANK % S
                pe.wait_ge(s["k_relued"], ch + 1 if side[ch] is main[ch] else ch)
                for i in range(4):
                    o = side[ch][:, P * i:P * (i + 1)]
                    t1 = t0 + P * i
                    pe.matmul(o, x1T[:, b, 1 + t1:1 + t1 + P], w_cur[:, 0, :], start=True, stop=False)
                    last = pe.matmul(o, x1T[:, b, t1:t1 + P], w_prev[:, 0, :], start=False, stop=True)
                last.then_inc(s["r_scored"], 1)

            def ffn_o(ch):
                if side[ch] is main[ch]:
                    pe.wait_ge(s["r_gated"], ch + 1)
                pe.wait_ge(s["k_squared"], ch + 1)
                for i in range(4):
                    last = pe.matmul(main[ch][:, P * i:P * (i + 1)], k_act[:, ch % 2, P * i:P * (i + 1)], wvT[:],
                                     start=True, stop=True)
                last.then_inc(s["o_scored"], 1)

            beside = {(NG - 2, 8): [(turn_attn, 0), (turn_attn, 1)], (NG - 2, 9): [(project, 0), (project, 1)],
                      (NG - 1, 2): [(turn_x1, 0)], (NG - 1, 3): [(ffn_k, 0)],
                      (NG - 1, 4): [(ffn_r, 0), (turn_x1, 1)], (NG - 1, 5): [(ffn_k, 1), (ffn_o, 0)],
                      (NG - 1, 6): [(ffn_r, 1)], (NG - 1, 9): [(ffn_o, 1)]}

            def group(n, par):
                static = isinstance(n, int)
                for k in range(NQ):
                    if k < TQUAD:
                        units = [] if static and n + 1 >= NG else \
                            [(n + 1, 1 - par, EARLY + sum(UNITS_AT[:k]) + u) for u in range(UNITS_AT[k])]
                    else:
                        units = [] if static and n + 2 >= NG else \
                            [(n + 2, par, sum(UNITS_AT[TQUAD:k]) + u) for u in range(UNITS_AT[k])]
                    for u in units[:1]:
                        max_unit(*u)
                    score_pair(n, par, k, 0)
                    for u in units[1:2]:
                        max_unit(*u)
                    score_pair(n, par, k, 1)
                    for half in range(2):
                        for u in units[2 + half:3 + half] if k != TQUAD or half else []:
                            max_unit(*u)
                        if k >= LAG:
                            sum_part(n, par, k - LAG, half, len(units) < 4)
                        elif not (static and n == 0):
                            sum_part(n - 1, 1 - par, NQ - LAG + k, half, len(units) < 4)
                        if k == TQUAD and half == 0:
                            if not (static and n + 1 >= NG):
                                turn_maxima(n + 1, 1 - par)
                            for u in units[2:3]:
                                max_unit(*u)
                    if k == LAG and not (static and n == 0):
                        turn_sums(n - 1, 1 - par)
                    if k == 3 + LAG and static and n == NG - 1:
                        turn_sums(n, par)
                    if static:
                        for stage, ch in beside.get((n, k), []):
                            stage(ch)

            group(0, 0)
            group(1, 1)
            with pe.Fori(1, NG // 2 - 1) as i:
                group(2 * i, 0)
                group(2 * i + 1, 1)
            group(NG - 2, 0)
            group(NG - 1, 1)
            sum_part(NG - 1, 1, NQ - 2, 0, True)
            turn_attn(2)
            sum_part(NG - 1, 1, NQ - 1, 0, True)
            turn_sums(NG, 0)
            project(2)
            turn_attn(3)
            project(3)
            for ch in (2, 3):
                turn_x1(ch)
                ffn_k(ch)
                ffn_r(ch)
                ffn_o(ch)

        @block.scalar
        def _(act):
            for weights, source in ((wq_sb, Wq), (wk_sb, Wk)):
                act.dma_start(weights[:], source).then_inc(s["wqk_in"], 16)
            act.dma_start(wv_sb[:], Wv).then_inc(s["wv_in"], 16)

            def copy_x(ch):
                act.wait_ge(s["xt_done"], ch + 1)
                nc.scalar.copy(xT[:, BANK * ch:BANK * (ch + 1)], wide[ch]).then_inc(s["xt_copied_a"], 1)

            def high(m):
                act.wait_ge(s["proj_done"], m + 1)
                hi = parts[m % 2][0][:].rearrange("p b t -> p (b t)")[:, BANK * (m // 2):BANK * (m // 2 + 1)]
                nc.scalar.activation(hi,
                                     narrow[m % 4], ACT.Copy, scale=SCALE if m % 2 == 0 else 1.0)\
                    .then_inc(s["hi_done"], 1)

            def middle(m):
                act.wait_ge(s["rest_done"], m + 1)
                nc.scalar.copy(parts[m % 2][1][:].rearrange("p b t -> p (b t)")[:, BANK * (m // 2):BANK * (m // 2 + 1)],
                               rest[:, m % 4, :]).then_inc(s["mid_done"], 1)

            for b in range(B):
                copy_x(2 * b)
                high(4 * b)
                for m in range(4 * b + 1, 4 * b + 4):
                    high(m)
                    middle(m - 1)
                middle(4 * b + 3)
            for ch in range(NCH):
                b, kb = ch // 2, ch % 2 * 4
                act.wait_ge(s["v_done"], ch + 1)
                src = wide[ch].rearrange("p (k g w) -> p k g w", k=4, g=GPB)
                dst = v_all[:].rearrange("p (b g k w) -> p b k g w", b=B, g=GPB, k=NB)[:, b, kb:kb + 4]
                nc.scalar.copy(dst, src).then_inc(s["v_copied"], 1)
            act.wait_ge(s["lam_dots"], 2)
            nc.scalar.activation(lam_exp[:], lam_sum[:], ACT.Exp).then_inc(s["lam_exped"], 1)
            act.wait_ge(s["wt_done"], 1)
            nc.scalar.activation(wvT[:], wide[0][:, 2 * P:3 * P], ACT.Copy, scale=0.5)
            act.wait_ge(s["mu_ready"], 1)
            for i in range(2):
                src = wide[0][:, P * i:P * (i + 1)]
                nc.scalar.activation(w_cur[:, i, :], src, ACT.Copy, scale=mu[:, i:i + 1])
                last = nc.scalar.activation(w_prev[:, i, :], src, ACT.Copy, scale=mu1[:, i:i + 1])
            last.then_inc(s["wt_scaled"], 1)

            def take_sums(n, par, done=NQ):
                act.wait_ge(s["summed"], NQ * min(n, NG - 1) + done if isinstance(n, int) else NQ * n + done)
                wait(act, s["acc_turned"], n - 1)
                nc.scalar.copy(o_rows[par][:], acc[par][:]).then_inc(s["acc_copied"], 1)

            def store_sums(n, par):
                act.wait_ge(s["acc_turned"], n + 1)
                wait(act, s["norm_steps"], 9 * (n - 1))
                nc.scalar.copy(o_tok[par][:], acc[par][:].rearrange("p (a w) -> p a w", w=VPAD)[:, :, 0:VW + 1])\
                    .then_inc(s["o_stored"], 1)

            def store_chunk(c):
                act.wait_ge(s["acc_turned"], NG + c)
                act.wait_ge(s["norm_steps"], 9 * (NG - 2))
                turned = acc[1 - c][:].rearrange("p (a c w) -> p c a w", c=2, w=VPAD)
                nc.scalar.copy(o_tok[1][:].rearrange("p (a c) w -> p c a w", c=2)[:, c], turned[:, c, :, 0:VW + 1])\
                    .then_inc(s["o_stored"], 1)

            def copy_attn(ch):
                act.wait_ge(s["a_turned"], ch + 1)
                nc.scalar.copy(attnT[:, ch % 2, :], main[ch]).then_inc(s["a_copied"], 1)

            def copy_x1(ch):
                b, t0 = ch * BANK // S, ch * BANK % S
                act.wait_ge(s["x1_turned"], ch + 1)
                nc.scalar.copy(x1T[:, b, 1 + t0:1 + t0 + BANK], main[ch]).then_inc(s["x1_copied"], 1)

            def relu_k(ch):
                act.wait_ge(s["k_scored"], ch + 1)
                nc.scalar.activation(k_relu[:, ch % 2, :], main[ch], ACT.Relu).then_inc(s["k_relued"], 1)

            def gate_r(ch):
                act.wait_ge(s["r_scored"], ch + 1)
                nc.scalar.activation(r_tanh[:, ch % 2, :], side[ch], ACT.Tanh, scale=0.5).then_inc(s["r_gated"], 1)

            def apply_norm(src, rs, shift, dst, ch, shifted, ready):
                act.wait_ge(shifted, ch - 1)
                for i in range(4):
                    t = 4 * ch + i
                    last = nc.scalar.activation(dst[:, t, :], src[:, t, :], ACT.Identity, bias=shift[:, t:t + 1],
                                                scale=rs[:, t:t + 1])
                last.then_inc(ready, 1)

            def apply1(ch):
                apply_norm(y, rs1, shift1, x1, ch, s["shifted1"], s["x1_ready"])

            def apply2(ch):
                apply_norm(z, rs2, shift2, res, ch, s["shifted2"], s["out_ready"])

            beside = {(NG - 2, 8): [(copy_attn, 0), (copy_attn, 1)], (NG - 1, 2): [(copy_x1, 0)],
                      (NG - 1, 3): [(relu_k, 0)], (NG - 1, 4): [(gate_r, 0), (copy_x1, 1)],
                      (NG - 1, 5): [(relu_k, 1)], (NG - 1, 6): [(gate_r, 1)]}

            def group(n, par):
                static = isinstance(n, int)
                for k in range(NQ):
                    used = max(col + w for _, col, w in QUADS[k][1])
                    for p in range(2):
                        act.wait_ge(s["scored"], 2 * NQ * n + 2 * k + p + 1)
                        if p == 0:
                            wait(act, s["summed"], NQ * n + k - ESLOTS + 1)
                        nc.scalar.activation(e_buf[:, k % ESLOTS, 2 * p:2 * p + 2, 0:used], ex[p][:, :, 0:used],
                                             ACT.Exp).then_inc(s["exped"], 1)
                    if k == LAG - 1 and not (static and n == 0):
                        take_sums(n - 1, 1 - par)
                    if k == LAG + 1 and not (static and n == 0):
                        store_sums(n - 1, 1 - par)
                    if k == 2 + LAG and static and n == NG - 1:
                        take_sums(n, par, 3)
                    if k == 4 + LAG and static and n == NG - 1:
                        store_chunk(0)
                    if static:
                        for stage, ch in beside.get((n, k), []):
                            stage(ch)

            group(0, 0)
            group(1, 1)
            with act.Fori(1, NG // 2 - 1) as i:
                group(2 * i, 0)
                group(2 * i + 1, 1)
            group(NG - 2, 0)
            group(NG - 1, 1)
            copy_attn(2)
            take_sums(NG, 0)
            store_chunk(1)
            copy_attn(3)
            apply1(2)
            copy_x1(2)
            relu_k(2)
            apply1(3)
            gate_r(2)
            copy_x1(3)
            relu_k(3)
            gate_r(3)
            apply2(2)
            apply2(3)

        @block.vector
        def _(dve):
            def copy_x(ch):
                dve.wait_ge(s["xt_done"], ch + 1)
                nc.vector.tensor_copy(xT[:, BANK * ch:BANK * (ch + 1)], wide[ch]).then_inc(s["xt_copied_d"], 1)

            def remainder(m):
                dve.wait_ge(s["hi_done"], m + 1)
                wait(dve, s["lo_done"], m - 3)
                hi = parts[m % 2][0][:].rearrange("p b t -> p (b t)")[:, BANK * (m // 2):BANK * (m // 2 + 1)]
                nc.vector.scalar_tensor_tensor(out=rest[:, m % 4, :], in0=narrow[m % 4],
                                               scalar=SCALE if m % 2 == 0 else 1.0, in1=hi, op0=ALU.mult,
                                               op1=ALU.subtract).then_inc(s["rest_done"], 1)

            def low(m):
                dve.wait_ge(s["mid_done"], m + 1)
                cols = slice(BANK * (m // 2), BANK * (m // 2 + 1))
                mid, lo = (parts[m % 2][a][:].rearrange("p b t -> p (b t)")[:, cols] for a in (1, 2))
                nc.vector.tensor_tensor(lo, rest[:, m % 4, :], mid, ALU.subtract).then_inc(s["lo_done"], 1)

            for b in range(B):
                copy_x(2 * b + 1)
                remainder(4 * b)
                for m in range(4 * b + 1, 4 * b + 4):
                    remainder(m)
                    low(m - 1)
                low(4 * b + 3)
            dve.wait_ge(s["small_in"], 16 * 6)
            nc.vector.tensor_tensor(lam_prod[:], lam_in[:, 0:2, :], lam_in[:, 2:4, :], ALU.mult)\
                .then_inc(s["lam_dots"], 1)
            dve.wait_ge(s["lam_dots"], 1)
            nc.vector.tensor_reduce(lam_sum[:], lam_prod[:], AX.X, ALU.add).then_inc(s["lam_dots"], 1)
            nc.vector.tensor_scalar(mu1[:], mu[:], -1.0, 1.0, ALU.mult, ALU.add).then_inc(s["mu_ready"], 1)
            dve.wait_ge(s["lam_exped"], 1)
            nc.vector.scalar_tensor_tensor(out=lam_neg[:], in0=lam_exp[:, 1:2], scalar=-LAMBDA_INIT,
                                           in1=lam_exp[:, 0:1], op0=ALU.add, op1=ALU.subtract)\
                .then_inc(s["lam_done"], 1)
            dve.wait_ge(s["lam_done"], 1)
            lam_view = lam_pair[:].rearrange("p (a s c) -> p s a c", s=2, c=2)
            nc.vector.memset(lam_view[:, 0], 1.0).then_inc(s["lam_paired"], 1)
            nc.vector.tensor_copy(lam_view[:, 1], lam_neg[:].unsqueeze(2).broadcast_to([P, NB * SUBS // 4, 2]))\
                .then_inc(s["lam_paired"], 1)
            def max_unit(n, par, k):
                dve.wait_ge(s["max_scored"], NU * n + k + 1)
                u, j = divmod(k, SUBS)
                if k == 0:
                    wait(dve, s["negmax_done"], n)
                target = ([part_max[:, j, 0, :], part_max[:, j, 1, :], row_max[:, j, 3:4], row_max[:, j, 7:8]]
                          + [far_max[:, j, i:i + 1] for i in range(4)] + [row_max[:, j, 1:8:4]])[u]
                nc.vector.tensor_reduce(target, mx[k % 2][:].rearrange("p (a b) -> p a b", a=target.shape[1]),
                                        AX.X, ALU.max).then_inc(s["maxed"], 1)

            def copy_maxima(n, par):
                wait(dve, s["max_rows_in"], 32 * n)
                dve.wait_ge(s["negmax_turned"], n + 1)
                nc.vector.tensor_copy(max_rows[:], acc[par][0:2 * SUBS, :].bitcast(BF16))\
                    .then_inc(s["negmax_copied"], 1)

            def combine(n):
                dve.wait_ge(s["maxed"], NU * (n + 1))
                wait(dve, s["negmax_done"], n)
                wait(dve, s["negmax_turned"], n)
                nc.vector.tensor_reduce(row_max[:, :, 2:8:4], part_max[:, :, :, 0:3], AX.X, ALU.max)\
                    .then_inc(s["combined"], 1)
                nc.vector.tensor_copy(row_max[:, :, 0:8:4], part_max[:, :, :, 3]).then_inc(s["combined"], 1)
                dve.wait_ge(s["combined"], 2 * n + 2)
                nc.vector.tensor_tensor(row_max[:, :, 4:8], row_max[:, :, 4:8], far_max[:], ALU.max)\
                    .then_inc(s["normed_d"], 1)
                dve.wait_ge(s["normed_d"], 2 * n + 1)
                nc.vector.tensor_scalar(neg_max[:, 0], row_max[:], -1.0, None, ALU.mult).then_inc(s["normed_d"], 1)
                dve.wait_ge(s["normed_d"], 2 * n + 2)
                nc.vector.scalar_tensor_tensor(out=neg_max[:, 1], in0=row_max[:], scalar=-1.0,
                                               in1=neg_max[:, 0], op0=ALU.mult, op1=ALU.subtract)\
                    .then_inc(s["negmax_done"], 1)

            for k in range(NU):
                max_unit(0, 0, k)
            combine(0)
            max_unit(1, 1, 0)
            max_unit(1, 1, 1)
            copy_maxima(0, 0)
            for k in range(2, EARLY):
                max_unit(1, 1, k)
            dve.wait_ge(s["rms_in"], 16)
            nc.vector.tensor_scalar(rms_scaled[:], rms_col[:], (1.0 - LAMBDA_INIT) * VW ** 0.5, None, ALU.mult)\
                .then_inc(s["rms_done"], 1)
            dve.wait_ge(s["rms_done"], 1)
            dve.wait_ge(s["w_in"], 16 * 4)
            nc.vector.tensor_scalar(wo_scaled[:], wo_sb[:], rms_scaled[:], None, ALU.mult).then_inc(s["rms_done"], 1)

            def invert(n, par):
                dve.wait_ge(s["o_stored"], n + 1)
                wait(dve, s["norm_steps"], 9 * (n - 1))
                nc.vector.reciprocal(r_den[par][:], o_tok[par][:, :, VW])\
                    .then_inc(s["den_inverted"], 1)

            def group(n, par):
                static = isinstance(n, int)
                if not (static and n + 1 >= NG):
                    for k in range(EARLY, NU):
                        max_unit(n + 1, 1 - par, k)
                        if k == EARLY + sum(UNITS_AT[:4]) and not (static and n == 0):
                            invert(n - 1, 1 - par)
                    combine(n + 1)
                if not (static and n + 2 >= NG):
                    for k in range(TURNED):
                        max_unit(n + 2, par, k)
                if not (static and n + 1 >= NG):
                    copy_maxima(n + 1, 1 - par)
                if not (static and n + 2 >= NG):
                    for k in range(TURNED, EARLY):
                        max_unit(n + 2, par, k)

            group(0, 0)
            group(1, 1)
            with dve.Fori(1, NG // 2 - 1) as i:
                group(2 * i, 0)
                group(2 * i + 1, 1)
            group(NG - 2, 0)

            def norm_stats(src, st, mv, ve, nm, ch, stats):
                for i in range(4):
                    nc.vector.bn_stats(st[:, 4 * ch + i, :], src[:, 4 * ch + i, :]).then_inc(stats, 1)
                dve.wait_ge(stats, 9 * ch + 4)
                for i in range(4):
                    nc.vector.bn_aggr(mv[:, 4 * ch + i, :], st[:, 4 * ch + i, :]).then_inc(stats, 1)
                dve.wait_ge(stats, 9 * ch + 8)
                tiles = slice(4 * ch, 4 * ch + 4)
                if ch >= NCH // B:
                    nc.vector.tensor_scalar(nm[:, tiles], mv[:, tiles, 0], -1.0, None, ALU.mult)
                nc.vector.tensor_scalar(ve[:, tiles], mv[:, tiles, 1], LN_EPS, None, ALU.add).then_inc(stats, 1)

            def apply_norm(src, mv, rs, dst, ch, rooted, ready):
                dve.wait_ge(rooted, ch + 1)
                for i in range(4):
                    t = 4 * ch + i
                    last = nc.vector.tensor_scalar(dst[:, t, :], src[:, t, :], mv[:, t, 0:1], rs[:, t:t + 1],
                                                   ALU.subtract, ALU.mult)
                last.then_inc(ready, 1)

            def apply1(ch):
                apply_norm(y, mv1, rs1, x1, ch, s["rooted1"], s["x1_ready"])

            def apply2(ch):
                apply_norm(z, mv2, rs2, res, ch, s["rooted2"], s["out_ready"])

            def norm_attn(ch):
                dve.wait_ge(s["a_projected"], ch + 1)
                nc.vector.tensor_tensor(y[:, 4 * ch:4 * ch + 4, :], main[ch].rearrange("p (t c) -> p t c", t=4),
                                        x_tok[:, 4 * ch:4 * ch + 4, :], ALU.add).then_inc(s["y_added"], 1)
                dve.wait_ge(s["y_added"], ch + 1)
                norm_stats(y, st1, mv1, ve1, nm1, ch, s["stats1"])

            def square_k(ch):
                dve.wait_ge(s["k_relued"], ch + 1)
                nc.vector.tensor_tensor(k_act[:, ch % 2, :], k_relu[:, ch % 2, :], k_relu[:, ch % 2, :], ALU.mult)\
                    .then_inc(s["k_squared"], 1)

            def norm_ffn(ch):
                dve.wait_ge(s["o_scored"], ch + 1)
                dve.wait_ge(s["r_gated"], ch + 1)
                nc.vector.scalar_tensor_tensor(out=z0[:, ch % 2, :], in0=r_tanh[:, ch % 2, :], scalar=1.0,
                                               in1=main[ch], op0=ALU.add, op1=ALU.mult)\
                    .then_inc(s["z_scaled"], 1)
                dve.wait_ge(s["z_scaled"], ch + 1)
                nc.vector.tensor_tensor(z[:, 4 * ch:4 * ch + 4, :], z0[:, ch % 2, :].rearrange("p (t c) -> p t c", t=4),
                                        x1[:, 4 * ch:4 * ch + 4, :], ALU.add).then_inc(s["z_ready"], 1)
                dve.wait_ge(s["z_ready"], ch + 1)
                norm_stats(z, st2, mv2, ve2, nm2, ch, s["stats2"])

            def normalise_half(c):
                def seen(i):
                    dve.wait_ge(s["half_steps"], 7 * c + i)

                dve.wait_ge(s["o_stored"], NG + c)
                if c == 0:
                    dve.wait_ge(s["attn_ready"], 2 * (NG - 1))
                nc.vector.reciprocal(r_den[1][:, c::2], o_tok[1][:, c::2, VW]).then_inc(s["half_steps"], 1)
                seen(1)
                nc.vector.tensor_tensor(r_lam[:, c::2], r_den[1][:, c::2], lam_pair[:, c::2], ALU.mult)\
                    .then_inc(s["half_steps"], 1)
                seen(2)
                nc.vector.tensor_tensor(o_scaled[:, c::2], o_tok[1][:, c::2, 0:VW],
                                        r_lam[:, c::2].unsqueeze(2).broadcast_to([P, NB * SUBS // 2, VW]),
                                        ALU.mult).then_inc(s["half_steps"], 1)
                seen(3)
                nc.vector.tensor_tensor(attn[:, c::2], pairs[:, :, 0, VW * c:VW * (c + 1)],
                                        pairs[:, :, 1, VW * c:VW * (c + 1)], ALU.add).then_inc(s["half_steps"], 1)
                seen(4)
                nc.vector.tensor_tensor(attn_sq[:, c::2], attn[:, c::2], attn[:, c::2], ALU.mult)\
                    .then_inc(s["half_steps"], 1)
                seen(5)
                nc.vector.tensor_reduce(sq1[:, c::2], attn_sq[:, c::2], AX.X, ALU.add).then_inc(s["half_steps"], 1)
                seen(6)
                nc.vector.tensor_scalar(sq_eps[:, c::2], sq1[:, c::2], VW * RMS_EPS, None, ALU.add)\
                    .then_inc(s["half_steps"], 1)

            def place_half(c):
                dve.wait_ge(s["half_rooted"], c + 1)
                nc.vector.tensor_tensor(attn_out[:, NG - 1, c], attn_chunks[:, c], r_rms_chunks[:, c], ALU.mult)\
                    .then_inc(s["attn_ready"], 1)

            norm_attn(0)
            apply1(0)
            norm_attn(1)
            apply1(1)
            invert(NG - 2, 0)
            square_k(0)
            norm_ffn(0)
            apply2(0)
            normalise_half(0)
            square_k(1)
            place_half(0)
            norm_ffn(1)
            normalise_half(1)
            norm_attn(2)
            place_half(1)
            apply2(1)
            norm_attn(3)
            for ch in (2, 3):
                square_k(ch)
                norm_ffn(ch)


_INS = ["L0_attn_x", "L0_attn_Wq", "L0_attn_Wk", "L0_attn_Wv", "L0_attn_Wo", "L0_attn_lq1", "L0_attn_lk1",
        "L0_attn_lq2", "L0_attn_lk2", "L0_attn_rms_w", "L0_ffn_W_r", "L0_ffn_W_k", "L0_ffn_W_v",
        "L0_ffn_mu_r", "L0_ffn_mu_k"]


def kernel(**inputs):
    import numpy as _np
    import concourse.bacc as _bacc
    from concourse import mybir as _mybir
    from concourse.bass_utils import run_bass_kernel_spmd as _run

    nc = _bacc.Bacc("TRN2", target_bir_lowering=False, num_devices=1)
    arrays, args = {}, []
    for name in _INS:
        a = _np.ascontiguousarray(inputs[name])
        arrays[f"in_{name}"] = a
        args.append(nc.dram_tensor(f"in_{name}", a.shape, _mybir.dt.from_np(a.dtype), kind="ExternalInput").ap())
    shape = inputs["L0_attn_x"].shape
    args.append(nc.dram_tensor("out_0", shape, _mybir.dt.float32, kind="ExternalOutput").ap())
    build(nc, *args)
    r = _run(nc, [arrays], core_ids=[0])
    return r.results[0]["out_0"]
```
